# Optimizing a Trainium2 kernel written in Bass

```python
import numpy as np
import jax
import jax.numpy as jnp

def _softmax(x, axis=-1):
    return jax.nn.softmax(x, axis=axis)

def _gelu(x):
    return jax.nn.gelu(x, approximate=True)

def _silu(x):
    return jax.nn.silu(x)

def _sigmoid(x):
    return jax.nn.sigmoid(x)

def _layernorm(x, axis=-1, eps=1e-05):
    m = jnp.mean(x, axis=axis, keepdims=True)
    v = jnp.var(x, axis=axis, keepdims=True)
    return (x - m) / jnp.sqrt(v + eps)

def _scatter_add(tgt, idx, src, axis=0):
    return tgt.at[idx].add(src)

def _segment_sum(src, seg, n):
    return jax.ops.segment_sum(src, seg, n)
kernel_name = 'mk_adaln_d1_jaxref_r8_48aafe'

def setup_inputs(seed: int=0):
    np.random.seed(seed)
    _w = jnp.asarray

    def _L0_attn_setup():
        import jax, jax.numpy as jnp
        import numpy as np
        D_MODEL = 128
        NUM_HEADS = 16
        HEAD_DIM = D_MODEL // NUM_HEADS
        key = jax.random.key(seed)
        ks = jax.random.split(key, 5)
        B, S = (1, 512)
        scale = 0.02
        return {'x': jax.random.normal(ks[0], (B, S, D_MODEL), dtype=jnp.float32), 'w_q': jax.random.normal(ks[1], (D_MODEL, D_MODEL), dtype=jnp.float32) * scale, 'w_k': jax.random.normal(ks[2], (D_MODEL, D_MODEL), dtype=jnp.float32) * scale, 'w_v': jax.random.normal(ks[3], (D_MODEL, D_MODEL), dtype=jnp.float32) * scale, 'w_o': jax.random.normal(ks[4], (D_MODEL, D_MODEL), dtype=jnp.float32) * scale}
    _L0_attn_in = _L0_attn_setup()

    def _L0_ffn_setup():
        import jax, jax.numpy as jnp
        import numpy as np
        E = 8
        TOP_K = 2
        ROUTE_SCALE = 1.0
        ALPHA = 1.702
        LIMIT = 7.0
        D = 128
        F = 128
        B, S = (2, 128)

        def swiglu(h):
            g = jnp.minimum(h[..., ::2], LIMIT)
            l = jnp.clip(h[..., 1::2], -LIMIT, LIMIT)
            return g * jax.nn.sigmoid(ALPHA * g) * (l + 1.0)
        if __name__ == '__main__':
            out = reference(**setup_inputs())
            print(out.shape, out.dtype)
        key = jax.random.key(seed)
        ks = jax.random.split(key, 16)
        sd = 1.0 / np.sqrt(D)
        sf = 1.0 / np.sqrt(F)
        return {'x': jax.random.normal(ks[0], (B, S, D), jnp.float32), 'gate_w': jax.random.normal(ks[1], (E, D), jnp.float32) * sd, 'gate_b': jax.random.normal(ks[2], (E,), jnp.float32) * 0.01, 'w1': jax.random.normal(ks[3], (E, 2 * F, D), jnp.float32) * sd, 'b1': jax.random.normal(ks[4], (E, 2 * F), jnp.float32) * 0.01, 'w3': jax.random.normal(ks[5], (E, 2 * F, D), jnp.float32) * sd, 'b3': jax.random.normal(ks[6], (E, 2 * F), jnp.float32) * 0.01, 'w2': jax.random.normal(ks[7], (E, D, F), jnp.float32) * sf, 'b2': jax.random.normal(ks[8], (E, D), jnp.float32) * 0.01, 'sw1': jax.random.normal(ks[9], (2 * F, D), jnp.float32) * sd, 'sb1': jax.random.normal(ks[10], (2 * F,), jnp.float32) * 0.01, 'sw3': jax.random.normal(ks[11], (2 * F, D), jnp.float32) * sd, 'sb3': jax.random.normal(ks[12], (2 * F,), jnp.float32) * 0.01, 'sw2': jax.random.normal(ks[13], (D, F), jnp.float32) * sf, 'sb2': jax.random.normal(ks[14], (D,), jnp.float32) * 0.01}
    _L0_ffn_in = _L0_ffn_setup()
    _L0_c = _w((lambda *s: np.random.randn(*s).astype(np.float32) * 0.05)(8, 128))
    _L0_wmod = _w((lambda *s: np.random.randn(*s).astype(np.float32) * 0.05)(128, 6 * 128) * 128 ** (-0.5))
    _d = {'L0_attn_x': _L0_attn_in['x'], 'L0_attn_w_q': _L0_attn_in['w_q'], 'L0_attn_w_k': _L0_attn_in['w_k'], 'L0_attn_w_v': _L0_attn_in['w_v'], 'L0_attn_w_o': _L0_attn_in['w_o'], 'L0_ffn_gate_w': _L0_ffn_in['gate_w'], 'L0_ffn_gate_b': _L0_ffn_in['gate_b'], 'L0_ffn_w1': _L0_ffn_in['w1'], 'L0_ffn_b1': _L0_ffn_in['b1'], 'L0_ffn_w3': _L0_ffn_in['w3'], 'L0_ffn_b3': _L0_ffn_in['b3'], 'L0_ffn_w2': _L0_ffn_in['w2'], 'L0_ffn_b2': _L0_ffn_in['b2'], 'L0_ffn_sw1': _L0_ffn_in['sw1'], 'L0_ffn_sb1': _L0_ffn_in['sb1'], 'L0_ffn_sw3': _L0_ffn_in['sw3'], 'L0_ffn_sb3': _L0_ffn_in['sb3'], 'L0_ffn_sw2': _L0_ffn_in['sw2'], 'L0_ffn_sb2': _L0_ffn_in['sb2'], 'L0_c': _L0_c, 'L0_wmod': _L0_wmod}
    _x0 = _d['L0_attn_x']
    _d['L0_attn_x'] = jax.random.normal(jax.random.fold_in(jax.random.key(seed), 1), (8, 256, 128), dtype=_x0.dtype)
    del _x0
    return _d

def reference(L0_attn_x, L0_attn_w_q, L0_attn_w_k, L0_attn_w_v, L0_attn_w_o, L0_ffn_gate_w, L0_ffn_gate_b, L0_ffn_w1, L0_ffn_b1, L0_ffn_w3, L0_ffn_b3, L0_ffn_w2, L0_ffn_b2, L0_ffn_sw1, L0_ffn_sb1, L0_ffn_sw3, L0_ffn_sb3, L0_ffn_sw2, L0_ffn_sb2, L0_c, L0_wmod):

    def _L0_attn_ref(x, w_q, w_k, w_v, w_o):
        import jax, jax.numpy as jnp
        import numpy as np
        D_MODEL = 128
        NUM_HEADS = 16
        HEAD_DIM = D_MODEL // NUM_HEADS
        B, S, _ = x.shape
        q = x @ w_q.T
        k = x @ w_k.T
        v = x @ w_v.T
        q = q.reshape(B, S, NUM_HEADS, HEAD_DIM)
        k = k.reshape(B, S, NUM_HEADS, HEAD_DIM)
        v = v.reshape(B, S, NUM_HEADS, HEAD_DIM)
        scale = HEAD_DIM ** (-0.5)
        scores = jnp.einsum('bqhd,bkhd->bhqk', q, k) * scale
        weights = jax.nn.softmax(scores, axis=-1)
        out = jnp.einsum('bhqk,bkhd->bqhd', weights, v)
        concat = out.reshape(B, S, D_MODEL)
        return concat @ w_o.T

    def _L0_ffn_ref(x, gate_w, gate_b, w1, b1, w3, b3, w2, b2, sw1, sb1, sw3, sb3, sw2, sb2):
        import jax, jax.numpy as jnp
        import numpy as np
        E = 8
        TOP_K = 2
        ROUTE_SCALE = 1.0
        ALPHA = 1.702
        LIMIT = 7.0
        D = 128
        F = 128
        B, S = (2, 128)

        def swiglu(h):
            g = jnp.minimum(h[..., ::2], LIMIT)
            l = jnp.clip(h[..., 1::2], -LIMIT, LIMIT)
            return g * jax.nn.sigmoid(ALPHA * g) * (l + 1.0)
        if __name__ == '__main__':
            out = reference(**setup_inputs())
            print(out.shape, out.dtype)
        inp_shape = x.shape
        xt = x.reshape(-1, D)
        logits = xt @ gate_w.T
        scores = jax.nn.softmax(logits.astype(jnp.float32), axis=-1)
        biased = scores + gate_b.astype(jnp.float32)
        idx = jax.lax.top_k(biased, TOP_K)[1]
        weights = (jnp.take_along_axis(scores, idx, axis=-1) * ROUTE_SCALE).astype(x.dtype)
        cw = jnp.sum(jax.nn.one_hot(idx, E, dtype=x.dtype) * weights[..., None], axis=1)
        h1 = jnp.einsum('td,efd->etf', xt, w1) + b1[:, None, :]
        h3 = jnp.einsum('td,efd->etf', xt, w3) + b3[:, None, :]
        a = swiglu(h1 * h3)
        y = jnp.einsum('etf,edf->etd', a, w2) + b2[:, None, :]
        routed = jnp.einsum('te,etd->td', cw, y)
        sh = swiglu((xt @ sw1.T + sb1) * (xt @ sw3.T + sb3))
        shared = sh @ sw2.T + sb2
        return (routed + shared).reshape(inp_shape)
    x = L0_attn_x
    mod = (_silu(L0_c) @ L0_wmod).reshape(L0_c.shape[0], 6, 1, -1)
    sa, ca, ga, sb, cb, gb = (mod[:, 0], mod[:, 1], mod[:, 2], mod[:, 3], mod[:, 4], mod[:, 5])
    ga = (2 * (ga >= 0) - 1) * jnp.maximum(jnp.abs(ga), 0.25)
    gb = (2 * (gb >= 0) - 1) * jnp.maximum(jnp.abs(gb), 0.25)
    h = _layernorm(x, axis=-1) * (1 + ca) + sa
    x = x + ga * _L0_attn_ref(h, L0_attn_w_q, L0_attn_w_k, L0_attn_w_v, L0_attn_w_o)
    h = _layernorm(x, axis=-1) * (1 + cb) + sb
    x = x + gb * _L0_ffn_ref(h, L0_ffn_gate_w, L0_ffn_gate_b, L0_ffn_w1, L0_ffn_b1, L0_ffn_w3, L0_ffn_b3, L0_ffn_w2, L0_ffn_b2, L0_ffn_sw1, L0_ffn_sb1, L0_ffn_sw3, L0_ffn_sb3, L0_ffn_sw2, L0_ffn_sb2)
    return x

_drawn_inputs = setup_inputs


def setup_inputs(seed=0):
    import zlib

    import numpy as np

    out = dict(_drawn_inputs(seed))
    spreads = {}
    factors = {'L0_attn_w_q': 8.0,
     'L0_attn_w_k': 8.0,
     'L0_attn_w_v': 8.0,
     'L0_attn_w_o': 8.0,
     'L0_ffn_gate_b': 4.806,
     'L0_ffn_b1': 48.615,
     'L0_ffn_b3': 47.13,
     'L0_ffn_b2': 60.085,
     'L0_ffn_sb1': 8.0,
     'L0_ffn_sb3': 22.643,
     'L0_ffn_sb2': 25.507}
    for name, (base, spread) in spreads.items():
        noise = np.random.default_rng([zlib.crc32(name.encode()), seed]).standard_normal(out[name].shape)
        drawn = base * np.exp(spread * noise) if base else spread * noise
        out[name] = jnp.asarray(drawn.astype(out[name].dtype))
    for name, factor in factors.items():
        out[name] = (out[name] * factor).astype(out[name].dtype)
    return out
```

```python
from contextlib import ExitStack

import concourse.bass as bass
from concourse import mybir


def block_kernel(nc, x_d, w4_d, cT_d, wmod_d, w13_d, w2_d, b13_d, b2_d, sb2_d, gw_d, gb_d, ident_d, cols_d, rev_d, y_d):
    fp32, f32r = mybir.dt.float32, mybir.dt.float32r
    ALU, ACT, AX = mybir.AluOpType, mybir.ActivationFunctionType, mybir.AxisListType
    P = 128
    D = x_d.shape[2]
    NT = x_d.shape[1]
    NB = cT_d.shape[1]
    TB = NT // NB
    S = TB * P
    HD = 8
    H = D // HD
    G = 4
    J = H // G
    SCALE = float(HD) ** -0.5
    EPS = 1e-5
    NE = gw_d.shape[1]
    NX = NE + 1
    CT = 4
    CW = CT * P
    NC = NT // CT
    ALPHA, LIMIT = 1.702, 7.0
    SLOTS = H
    DMA = 16

    cwd = nc.dram_tensor("cw_scratch", (NE, NT * P), fp32, kind="Internal").ap()

    ctx = ExitStack()
    with ctx:
        def sb(name, shape, dt=fp32):
            return ctx.enter_context(nc.sbuf_tensor(name, shape, dt))

        def sem(name):
            return ctx.enter_context(nc.semaphore(name))

        xs = sb("xs", [P, NT, D])
        w4 = sb("w4", [P, 4, P])
        w4h = sb("w4h", [P, 4, P], f32r)
        w4l = sb("w4l", [P, 4, P], f32r)
        wrep = [sb(f"wrep{n}", [P, 2, H, 4, HD], f32r) for n in range(2)]
        cT = sb("cT", [P, NB])
        sigc = sb("sigc", [P, NB])
        siluT = sb("siluT", [P, NB])
        gaB = sb("gaB", [P, NB, P])
        mod = sb("mod", [P, 6, NB])
        mod1 = sb("mod1", [P, 6, NB])
        gneg = sb("gneg", [P, 2, NB])
        gabs = sb("gabs", [P, 2, NB])
        gsgn = sb("gsgn", [P, 2, NB])
        gt = sb("gt", [P, 2, NB])
        gb_t = gt[:, 1, :]
        gbias = sb("gbias", [P, NB])
        ga_b = sb("ga_b", [P, NB, D])
        st1 = sb("st1", [P, NT, 6])
        mv1 = sb("mv1", [P, NT, 2])
        std1 = sb("std1", [P, NT])
        rstd1 = sb("rstd1", [P, NT])
        ident = sb("ident", [P, P])
        cols = sb("cols", [P, 3 + J])
        rev = sb("rev", [P, NE])
        zcol = sb("zcol", [P, 1])
        xn = sb("xn", [P, TB, D])
        hf = sb("hf", [P, S])
        hh = [sb(f"hh{n}", [P, S], f32r) for n in range(2)]
        hl = [sb(f"hl{n}", [P, S], f32r) for n in range(2)]
        hiS = [sb(f"hiS{n}", [P, 2, S], f32r) for n in range(2)]
        stage = sb("stage", [P, 2, G, S], f32r)
        Qst = [sb(f"Qst{n}", [P, G, S], f32r) for n in range(2)]
        Kx = sb("Kx", [P, 2, H, S], f32r)
        Vb = sb("Vb", [P, 2, TB, H, 32])
        V = [Vb[:, n] for n in range(2)]
        M = sb("M", [P, 2, TB, H])
        mhl = sb("mhl", [8, 2, 2, S], f32r)
        OT = sb("OT", [P, G, S])
        rd = sb("rd", [P, H])
        cc = sb("cc", [P, TB, D])
        cch = sb("cch", [P, S], f32r)
        ccl = sb("ccl", [P, S], f32r)
        rt = sb("rt", [P, TB, D])
        st2 = sb("st2", [P, NT, 6])
        mv2 = sb("mv2", [P, NT, 2])
        std2 = sb("std2", [P, NT])
        rstd2 = sb("rstd2", [P, NT])
        w13h = sb("w13h", [P, NX, 4 * P], f32r)
        w13l = sb("w13l", [P, NX, 4 * P], f32r)
        w2 = sb("w2", [P, NX, P])
        b13 = sb("b13", [P, NX, 4])
        b2 = sb("b2", [P, D])
        sb2 = sb("sb2", [P, 1])
        gwT = sb("gwT", [P, NE])
        gwh = sb("gwh", [P, NE], f32r)
        gwl = sb("gwl", [P, NE], f32r)
        gbb = sb("gbb", [P, NE])
        NF = 21
        F = sb("F", [P, NF, CW])
        w13 = F[:, 0:NX, :]
        PE_RING = 8
        pt = [F[:, NX + n, :] for n in range(PE_RING)]
        R = 3
        t1g, t1l, pg, pl, X, sg, av = [[F[:, R * k + n, :] for n in range(R)] for k in range(7)]
        cwB = sb("cwB", [P, R, CW])
        H2h = Kx[:, 0, 0:H // 2, :].rearrange("p a b -> p (a b)")
        H2l = Kx[:, 0, H // 2:H, :].rearrange("p a b -> p (a b)")
        wmod = F[:, NX + PE_RING + 2:NX + PE_RING + 4, :].rearrange("p a b -> p (a b)")[:, 0:6 * D]\
            .rearrange("p (a b) -> p a b", a=6)
        cwT = Vb[:].rearrange("p a t h r -> p (a t h r)")
        xn2 = [OT[:, 0:2, :].rearrange("p a b -> p (a b)"), OT[:, 2:4, :].rearrange("p a b -> p (a b)")]
        hf2 = [gaB[:, 0:4, :].rearrange("p a b -> p (a b)"), gaB[:, 4:8, :].rearrange("p a b -> p (a b)")]
        zb = ga_b[:, 0:4, :].rearrange("p a b -> p (a b)")
        yo = ga_b[:, 4:8, :]
        lg = sb("lg", [P, NT, NE])
        sc = sb("sc", [P, NT, NE])
        bi = sb("bi", [P, NT, NE])
        eq = sb("eq", [P, NT, NE])
        oh = [sb(f"oh{n}", [P, NT, NE]) for n in range(2)]
        cw = sb("cw", [P, NT, NE])
        r1 = [sb(f"r1_{n}", [P, NT]) for n in range(7)]

        bank = [ctx.enter_context(nc.psum_tensor(f"bank{n}", [P, 512], fp32)) for n in range(8)]
        S_BANK, ST_BANK, PV_BANK, A_BANK, O_BANK, T_BANK = 0, 2, 4, 5, 6, 7
        Y_BANK, Z_BANK = 6, 7

        x_in = [sem(f"x_in{n}") for n in range(4)]
        c_in = sem("c_in")
        w4_in = sem("w4_in")
        cst_in = sem("cst_in")
        w13_in = sem("w13_in")
        small_in = sem("small_in")
        w2_in = sem("w2_in")
        dram_out = sem("dram_out")
        idle_zero = sem("idle_zero")
        b2_zero = sem("b2_zero")
        wsplit = sem("wsplit")
        wrep_done = sem("wrep_done")
        silu_sig = sem("silu_sig")
        silu_done = sem("silu_done")
        mod_mm = sem("mod_mm")
        mod_done = sem("mod_done")
        ga_mm = sem("ga_mm")
        g_chain = sem("g_chain")
        gaB_ready = sem("gaB_ready")
        ga_ready = sem("ga_ready")
        gb_ready = sem("gb_ready")
        gwsplit = sem("gwsplit")
        w13hi = sem("w13hi")
        w13lo = sem("w13lo")
        st1_done = sem("st1_done")
        mv1_done = sem("mv1_done")
        std_in = sem("std_in")
        std_done = sem("std_done")
        rstd_done = sem("rstd_done")
        xn_ready = sem("xn_ready")
        xnT_done = sem("xnT_done")
        h_ready = sem("h_ready")
        hl_ready = sem("hl_ready")
        qk_mm = sem("qk_mm")
        hi_ready = sem("hi_ready")
        stage_ready = sem("stage_ready")
        copied = sem("copied")
        s_mm = sem("s_mm")
        max_done = sem("max_done")
        mT_done = sem("mT_done")
        m_split = sem("m_split")
        mrow = [sem(f"mrow{n}") for n in range(2)]
        st_mm = sem("st_mm")
        exp_done = sem("exp_done")
        v_mm = sem("v_mm")
        v_ready = sem("v_ready")
        pv_mm = sem("pv_mm")
        ot_ready = sem("ot_ready")
        otr_mm = sem("otr_mm")
        rd_ready = sem("rd_ready")
        cc_ready = sem("cc_ready")
        cT_mm = sem("cT_mm")
        cch_ready = sem("cch_ready")
        ccl_ready = sem("ccl_ready")
        o_mm = sem("o_mm")
        rt_ready = sem("rt_ready")
        x2_ready = sem("x2_ready")
        st2_done = sem("st2_done")
        mv2_done = sem("mv2_done")
        std2_in = sem("std2_in")
        std2_done = sem("std2_done")
        rstd2_done = sem("rstd2_done")
        xn2_ready = sem("xn2_ready")
        x2T_done = sem("x2T_done")
        h2_ready = sem("h2_ready")
        h2l_ready = sem("h2l_ready")
        gate_mm = sem("gate_mm")
        route = sem("route")
        exp_gate = sem("exp_gate")
        cw_done = sem("cw_done")
        cwT_zero = sem("cwT_zero")
        cwT_mm = sem("cwT_mm")
        cwT_done = sem("cwT_done")
        cwB_in = [sem(f"cwB_in{n}") for n in range(R)]
        g_mm = sem("g_mm")
        l_mm = sem("l_mm")
        t1g_ready = sem("t1g_ready")
        t1l_ready = sem("t1l_ready")
        pg_ready = sem("pg_ready")
        gm_ready = sem("gm_ready")
        pl_ready = sem("pl_ready")
        lc_ready = sem("lc_ready")
        sg_ready = sem("sg_ready")
        x_ready = sem("x_ready")
        yx_ready = sem("yx_ready")
        a_ready = sem("a_ready")
        w2_mm = sem("w2_mm")
        y_ready = sem("y_ready")
        z_ready = sem("z_ready")
        zT_done = sem("zT_done")
        yo_ready = sem("yo_ready")

        def later(value):
            return not isinstance(value, int) or value > 0

        block = ctx.enter_context(nc.Block())

        def x_before(c, n):
            return NE * c + (n - R if n >= R else n - R + 1)

        def bodies(e, body):
            for b in range(-2, 2):
                body(b, b % 2)
            with e.Fori(0, (NB - 4) // 2) as i:
                body(2 * i + 2, 0)
                body(2 * i + 3, 1)
            for b in range(NB - 2, NB):
                body(b, b % 2)

        def has(b, stage_of):
            return not isinstance(b, int) or 0 <= b + stage_of < NB

        def a_bank(b, n):
            return bank[(A_BANK, PV_BANK, O_BANK, T_BANK)[n] if isinstance(b, int) and b == 0 else A_BANK]

        FIRST = 4

        @block.sync
        def _(sp):
            sp.dma_start(cT[:], cT_d).then_inc(c_in, DMA)
            q = NT // 4
            for n in range(4):
                sp.dma_start(xs[:, n * q:(n + 1) * q, :], x_d[:, n * q:(n + 1) * q, :]).then_inc(x_in[n], DMA)
                if n == 0:
                    sp.dma_start(wmod, wmod_d).then_inc(c_in, DMA)
                    sp.dma_start(w4[:], w4_d).then_inc(w4_in, DMA)
                    for dst, src in ((ident, ident_d), (cols, cols_d), (rev, rev_d)):
                        sp.dma_start(dst[:], src).then_inc(cst_in, DMA)
            sp.wait_ge(b2_zero, 1)
            sp.dma_start(b2[0:NE, :], b2_d).then_inc(small_in, DMA)
            sp.dma_start(sb2[:], sb2_d).then_inc(small_in, DMA)
            sp.dma_start(gwT[:], gw_d).then_inc(small_in, DMA)
            sp.dma_start(gbb[:], gb_d.partition_broadcast(P)).then_inc(small_in, DMA)
            sp.dma_start(b13[:], b13_d).then_inc(small_in, DMA)
            sp.dma_start(w13, w13_d).then_inc(w13_in, DMA)
            sp.dma_start(w2[:], w2_d).then_inc(w2_in, DMA)

            def maxima_rows(b, par, half):
                sp.wait_ge(m_split, 4 * b + 2 * half + 2)
                for part in range(2):
                    for g2 in range(2):
                        sp.dma_start(Qst[par][24 + part:P:32, 2 * half + g2, :].bitcast(fp32),
                                    mhl[J * g2:J * g2 + J, half, part, :].bitcast(fp32)).then_inc(mrow[half], DMA)

            def body(b, par):
                if has(b, 0):
                    maxima_rows(b, par, 1)
                if has(b, 1):
                    maxima_rows(b + 1, 1 - par, 0)

            bodies(sp, body)

            sp.wait_ge(cwT_done, NC)
            sp.dma_start(cwd, cwT[0:NE, :]).then_inc(dram_out, DMA)
            sp.wait_ge(dram_out, DMA)

            def chunk(c):
                for n in range(1, NX):
                    r = n % R
                    if later(x_before(c, n)):
                        sp.wait_ge(x_ready, x_before(c, n))
                    sp.dma_start(cwB[:, r, :], cwd[n - 1, bass.ds(c * CW, CW)].partition_broadcast(P))\
                     .then_inc(cwB_in[r], DMA)

            def store(c):
                sp.wait_ge(yo_ready, c + 1)
                sp.dma_start(y_d[:, bass.ds(c * CT, CT), :], yo).then_inc(dram_out, DMA)

            chunk(0)
            with sp.Fori(1, NC) as c:
                chunk(c)
                store(c - 1)
            store(NC - 1)
            sp.wait_ge(dram_out, (NC + 1) * DMA)

        @block.gpsimd
        def _(pool):
            pool.memset(zcol[:], 0.0)
            for n in range(2):
                pool.memset(V[n], 0.0).then_inc(idle_zero, 1)
            pool.wait_ge(idle_zero, 2)
            for n in range(2):
                pool.memset(V[n][:, :, :, HD:HD + 1], 1.0).then_inc(idle_zero, 1)
            pool.memset(b2[:], 0.0).then_inc(b2_zero, 1)

            def split_w13(n):
                pool.wait_ge(w13_in, DMA)
                pool.tensor_scalar(w13h[:, n, :], w13[:, n, :], 1.0, 0.0, ALU.mult, ALU.add).then_inc(w13hi, 1)
                pool.wait_ge(w13hi, n + 1)
                pool.tensor_tensor(w13l[:, n, :], w13[:, n, :], w13h[:, n, :].bitcast(fp32), ALU.subtract)\
                 .then_inc(w13lo, 1)

            def copy_group(b, par, g, reuse):
                pool.wait_ge(stage_ready, 4 * b + (3 if g < 2 else 4))
                if reuse:
                    pool.wait_ge(st_mm, SLOTS * (b - 2) + J * g + J)
                pool.tensor_tensor(Qst[par][:, g, :], stage[:, 0, g, :].bitcast(fp32), zcol[:].to_broadcast([P, S]),
                                ALU.add)
                for j in range(J):
                    last = pool.tensor_scalar(Kx[:, par, J * g + j, :], stage[:, 1, g, :].bitcast(fp32),
                                           cols[:, 3 + j:4 + j], 0.0, ALU.mult, ALU.add)
                last.then_inc(copied, 1)

            pool.wait_ge(cst_in, 3 * DMA)

            def body(b, par):
                if has(b, 2):
                    for g in range(G):
                        copy_group(b + 2, par, g, has(b, 0))
                if isinstance(b, int):
                    for n in {-2: (0, 1), -1: (2,), 0: (3,), 1: (4,), NB - 2: (5, 6), NB - 1: (7, 8)}[b]:
                        split_w13(n)

            bodies(pool, body)

            pool.wait_ge(pv_mm, G * NB)
            pool.memset(cwT, 0.0).then_inc(cwT_zero, 1)

            def expert(c, n):
                r = n % R
                k = NX * c + n
                if n > 0:
                    pool.wait_ge(gm_ready, k + 1)
                    pool.wait_ge(cwB_in[r], DMA * (len(range(r or R, NX, R)) * c + len(range(r or R, n + 1, R))))
                    if later(k - R + 1):
                        pool.wait_ge(a_ready, k - R + 1)
                    pool.tensor_tensor(X[r], pg[r], cwB[:, r, :], ALU.mult).then_inc(x_ready, 1)

            def gate(c, n):
                r = n % R
                k = NX * c + n
                pool.wait_ge(yx_ready, k + 1)
                pool.wait_ge(sg_ready, k + 1)
                if later(k - R + 1):
                    pool.wait_ge(w2_mm, k - R + 1)
                pool.tensor_tensor(av[r], X[r], sg[r], ALU.mult).then_inc(a_ready, 1)

            def chunk(c):
                for n in range(NX):
                    expert(c, n)
                    if n > 0 or not (isinstance(c, int) and c == 0):
                        k = NX * c + n - 1
                        gate(c, n - 1) if n > 0 else gate(c - 1, NX - 1)

            chunk(0)
            with pool.Fori(1, NC) as c:
                chunk(c)
            gate(NC - 1, NX - 1)

        @block.scalar
        def _(act):
            act.wait_ge(c_in, 2 * DMA)
            act.activation(sigc[:], cT[:], ACT.Sigmoid).then_inc(silu_sig, 1)
            act.wait_ge(mod_mm, 1)
            act.activation(mod[:], bank[0][:, 0:6 * NB].rearrange("p (a b) -> p a b", a=6), ACT.Identity)\
             .then_inc(mod_done, 1)
            act.wait_ge(std_in, 1)
            act.activation(std1[:, 0:FIRST], std1[:, 0:FIRST], ACT.Sqrt).then_inc(std_done, 1)

            def normed(b, par):
                act.wait_ge(xnT_done, b + 1)
                if later(b):
                    act.wait_ge(hl_ready, b)
                src = bank[A_BANK][:, 0:S]
                act.activation(hf[:], src, ACT.Identity, bias=mod[:, 0, bass.ds(b, 1)],
                             scale=mod1[:, 1, bass.ds(b, 1)]).then_inc(h_ready, 1)
                act.activation(hh[par][:], src, ACT.Identity, bias=mod[:, 0, bass.ds(b, 1)],
                             scale=mod1[:, 1, bass.ds(b, 1)]).then_inc(h_ready, 1)

            def hi_part(b, n):
                act.wait_ge(qk_mm, 4 * b + n + 1)
                if later(4 * b + n - 1):
                    act.wait_ge(stage_ready, 4 * b + n - 1)
                act.activation(hiS[n % 2][:], a_bank(b, n)[:].rearrange("p (a b) -> p a b", a=2), ACT.Identity,
                             bias=cols[:, 2:3] if n >= 2 else 0.0).then_inc(hi_ready, 1)

            def values(b, par):
                act.wait_ge(v_mm, b + 1)
                if later(G * (b - 1)):
                    act.wait_ge(pv_mm, G * (b - 1))
                act.activation(V[par][:, :, :, 0:HD],
                             bank[A_BANK][:, 0:TB * D].rearrange("p (t h d) -> p t h d", t=TB, h=H), ACT.Identity)\
                 .then_inc(v_ready, 1)

            def exps(b, i):
                u = SLOTS * b + i
                act.wait_ge(st_mm, u + 1)
                if later(G * b + i // J - 1):
                    act.wait_ge(pv_mm, G * b + i // J - 1)
                act.activation(pt[i % PE_RING], bank[ST_BANK + i % 2][:], ACT.Exp, scale=SCALE)\
                 .then_inc(exp_done, 1)

            def attended(b, g):
                act.wait_ge(pv_mm, G * b + g + 1)
                if later(TB * b):
                    act.wait_ge(otr_mm, TB * b)
                act.activation(OT[:, g, :], bank[PV_BANK][:, (g % 2) * S:(g % 2 + 1) * S], ACT.Identity)\
                 .then_inc(ot_ready, 1)

            def concat_hi(b):
                act.wait_ge(cT_mm, b + 1)
                if later(b):
                    act.wait_ge(o_mm, b)
                act.activation(cch[:], bank[T_BANK][:, 0:S], ACT.Identity).then_inc(cch_ready, 1)

            act.wait_ge(cst_in, 3 * DMA)

            def body(b, par):
                for i in range(SLOTS):
                    if has(b, 0):
                        exps(b, i)
                    if i == 1 and has(b, -1):
                        attended(b - 1, G - 1)
                    if i == 2 and has(b, 2):
                        normed(b + 2, par)
                    if i in (4, 6, 8, 10) and has(b, 2):
                        hi_part(b + 2, (i - 4) // 2)
                    if i == 8 and has(b, -1):
                        concat_hi(b - 1)
                    if i in (6, 10, 14) and has(b, 0):
                        attended(b, (i - 6) // 4)
                    if i == 13 and has(b, 1):
                        if isinstance(b, int) and b == -1:
                            act.wait_ge(idle_zero, 4)
                        values(b + 1, 1 - par)
                    if i == SLOTS - 2 and isinstance(b, int) and b == -2:
                        act.wait_ge(std_in, 2)
                        act.activation(std1[:, FIRST:NT], std1[:, FIRST:NT], ACT.Sqrt).then_inc(std_done, 1)
                    if i == 5 and isinstance(b, int) and b == -1:
                        act.wait_ge(ga_mm, 1)
                        for k in range(2):
                            act.activation(ga_b[:, 4 * k:4 * k + 4, :].rearrange("p a b -> p (a b)"),
                                           bank[ST_BANK + k][:], ACT.Identity).then_inc(ga_ready, 1)

            bodies(act, body)
            attended(NB - 1, G - 1)
            concat_hi(NB - 1)

            act.wait_ge(small_in, 5 * DMA)
            act.wait_ge(std2_in, 1)
            act.activation(std2[:], std2[:], ACT.Sqrt).then_inc(std2_done, 1)
            for c in range(NC):
                act.wait_ge(x2T_done, c + 1)
                if c >= 2:
                    act.wait_ge(h2l_ready, c - 1)
                for k in range(CW // S):
                    b = c * (CW // S) + k
                    src = bank[c % 2][:, k * S:(k + 1) * S]
                    act.activation(hf2[c % 2][:, k * S:(k + 1) * S], src, ACT.Identity, bias=mod[:, 3, b:b + 1],
                                 scale=mod1[:, 4, b:b + 1])
                    act.activation(H2h[:, c * CW + k * S:c * CW + (k + 1) * S], src, ACT.Identity,
                                 bias=mod[:, 3, b:b + 1], scale=mod1[:, 4, b:b + 1]).then_inc(h2_ready, 1)
            act.wait_ge(route, 2)
            act.activation(sc[:], lg[:], ACT.Exp).then_inc(exp_gate, 1)
            act.wait_ge(cwT_zero, 1)
            for c in range(NC):
                act.wait_ge(cwT_mm, c + 1)
                act.activation(cwT[0:NE, c * CW:(c + 1) * CW], bank[c][0:NE, :], ACT.Identity)\
                 .then_inc(cwT_done, 1)

            def chunk(c):
                for n in range(NX):
                    r = n % R
                    k = NX * c + n
                    act.wait_ge(g_mm, k + 1)
                    if later(k - R + 1):
                        act.wait_ge(pg_ready, k - R + 1)
                    act.activation(t1g[r], bank[2 * ((2 * n) % R)][:], ACT.Identity, bias=b13[:, n, 0:1])\
                     .then_inc(t1g_ready, 1)
                    if n > 0 or not isinstance(c, int):
                        sigmoid(c, n - 1) if n > 0 else sigmoid(c - 1, NX - 1)
                    if n == 2 and not isinstance(c, int):
                        scaled(c - 1)
                    act.wait_ge(l_mm, k + 1)
                    if later(k - R + 1):
                        act.wait_ge(pl_ready, k - R + 1)
                    act.activation(t1l[r], bank[2 * ((2 * n + 1) % R)][:], ACT.Identity, bias=b13[:, n, 1:2])\
                     .then_inc(t1l_ready, 1)

            def sigmoid(c, n):
                k = NX * c + n
                act.wait_ge(gm_ready, k + 1)
                if later(k - R + 1):
                    act.wait_ge(a_ready, k - R + 1)
                act.activation(sg[n % R], pg[n % R], ACT.Sigmoid, scale=ALPHA).then_inc(sg_ready, 1)

            def scaled(c):
                act.wait_ge(y_ready, c + 1)
                for k in range(CW // S):
                    b = c * (CW // S) + k
                    last = act.activation(zb[:, k * S:(k + 1) * S], bank[Y_BANK][:, k * S:(k + 1) * S], ACT.Identity,
                                        bias=gbias[:, bass.ds(b, 1)], scale=gb_t[:, bass.ds(b, 1)])
                last.then_inc(z_ready, 1)

            chunk(0)
            with act.Fori(1, NC) as c:
                chunk(c)
            sigmoid(NC - 1, NX - 1)
            scaled(NC - 1)

        @block.vector
        def _(dve):
            dve.wait_ge(silu_sig, 1)
            dve.tensor_tensor(siluT[:], cT[:], sigc[:], ALU.mult).then_inc(silu_done, 1)
            def stats1(tiles):
                for n in tiles:
                    if n % 4 == 0:
                        dve.wait_ge(x_in[n // 4], DMA)
                    last = dve.bn_stats(st1[:, n, :], xs[:, n, :])
                last.then_inc(st1_done, 1)

            def variances(group, tiles):
                for n in tiles:
                    last = dve.bn_aggr(mv1[:, n, :], st1[:, n, :])
                last.then_inc(mv1_done, 1)
                dve.wait_ge(mv1_done, group + 1)
                dve.tensor_scalar(std1[:, tiles[0]:NT if group else FIRST], mv1[:, tiles[0]:NT if group else FIRST, 1],
                                  EPS, None, ALU.add).then_inc(std_in, 1)

            stats1(range(FIRST))
            dve.wait_ge(st1_done, 1)
            variances(0, range(FIRST))
            dve.wait_ge(w4_in, DMA)
            dve.tensor_copy(w4h[:], w4[:]).then_inc(wsplit, 1)
            dve.memset(wrep[0][:].bitcast(fp32), 0.0)
            dve.memset(wrep[1][:].bitcast(fp32), 0.0).then_inc(wsplit, 1)
            dve.wait_ge(std_done, 1)
            dve.reciprocal(rstd1[:, 0:FIRST], std1[:, 0:FIRST]).then_inc(rstd_done, 1)
            dve.wait_ge(wsplit, 2)
            dve.tensor_tensor(w4l[:], w4[:], w4h[:].bitcast(fp32), ALU.subtract).then_inc(wsplit, 1)
            dve.wait_ge(mod_done, 1)
            dve.tensor_scalar(mod1[:], mod[:], 1.0, None, ALU.add).then_inc(mod_done, 1)
            dve.wait_ge(rstd_done, 1)

            def normalise(b):
                if later(b):
                    dve.wait_ge(xnT_done, b)
                for k in range(TB):
                    t = TB * b + k
                    last = dve.tensor_scalar(xn[:, k, :], xs[:, bass.ds(t, 1), :].rearrange("p a d -> p (a d)"),
                                           mv1[:, bass.ds(t, 1), 0], rstd1[:, bass.ds(t, 1)],
                                           ALU.subtract, ALU.mult)
                last.then_inc(xn_ready, 1)

            def h_lo(b, par):
                dve.wait_ge(h_ready, 2 * b + 2)
                dve.tensor_tensor(hl[par][:], hf[:], hh[par][:].bitcast(fp32), ALU.subtract).then_inc(hl_ready, 1)

            def stacked(b, n):
                dve.wait_ge(hi_ready, 4 * b + n + 1)
                if later(G * b):
                    dve.wait_ge(copied, G * b)
                qk, half = n // 2, n % 2
                dve.scalar_tensor_tensor(out=stage[:, qk, 2 * half:2 * half + 2, :].rearrange("p a b -> p (a b)"),
                                       in0=hiS[n % 2][:].bitcast(fp32).rearrange("p a b -> p (a b)"),
                                       scalar=cols[:, qk:qk + 1], in1=a_bank(b, n)[:], op0=ALU.mult, op1=ALU.add)\
                 .then_inc(stage_ready, 1)

            def maximum(b, par, i):
                u = SLOTS * b + i
                dve.wait_ge(s_mm, u + 1)
                if i == 0:
                    if later(2 * (b - 1)):
                        dve.wait_ge(mT_done, 2 * (b - 1))
                dve.tensor_reduce(out=M[:, par, i % 2, 2 * (i // 2):2 * (i // 2) + 2],
                                in_=bank[S_BANK + i % 2][:].rearrange("p (a k) -> p a k", a=2),
                                axis=AX.X, op=ALU.max, negate=True).then_inc(max_done, 1)

            def maxima_parts(b, half):
                dve.wait_ge(mT_done, 2 * b + half + 1)
                if later(4 * DMA * b):
                    dve.wait_ge(mrow[half], 4 * DMA * b)
                dve.tensor_copy(mhl[:, half, 0, :], bank[T_BANK][0:8, 0:S]).then_inc(m_split, 1)
                dve.wait_ge(m_split, 4 * b + 2 * half + 1)
                dve.tensor_tensor(mhl[:, half, 1, :], bank[T_BANK][0:8, 0:S], mhl[:, half, 0, :].bitcast(fp32),
                                ALU.subtract).then_inc(m_split, 1)

            def divided(b, qt):
                dve.wait_ge(otr_mm, TB * b + qt + 1)
                if later(b):
                    dve.wait_ge(cT_mm, b)
                o = bank[O_BANK][:].rearrange("p (h r) -> p h r", h=H)
                dve.reciprocal(rd[:], o[:, :, HD]).then_inc(rd_ready, 1)
                dve.wait_ge(rd_ready, TB * b + qt + 1)
                dve.tensor_tensor(cc[:, qt, :].rearrange("p (h d) -> p h d", h=H), o[:, :, 0:HD],
                                rd[:].unsqueeze(2).to_broadcast([P, H, HD]), ALU.mult).then_inc(cc_ready, 1)

            def concat_lo(b):
                dve.wait_ge(cch_ready, b + 1)
                dve.tensor_tensor(ccl[:], bank[T_BANK][:, 0:S], cch[:].bitcast(fp32), ALU.subtract)\
                 .then_inc(ccl_ready, 1)

            def residual(b):
                dve.wait_ge(o_mm, b + 1)
                dve.tensor_tensor(rt[:], bank[O_BANK][:, 0:TB * D].rearrange("p (t d) -> p t d", t=TB),
                                ga_b[:, bass.ds(b, 1), :].to_broadcast([P, TB, D]), ALU.mult)\
                 .then_inc(rt_ready, 1)
                dve.wait_ge(rt_ready, b + 1)
                xt = xs[:, bass.ds(TB * b, TB), :]
                dve.tensor_tensor(xt, rt[:], xt, ALU.add).then_inc(x2_ready, 1)

            def stats2(b):
                dve.wait_ge(x2_ready, b + 1)
                for k in range(TB):
                    t = TB * b + k
                    last = dve.bn_stats(st2[:, bass.ds(t, 1), :].rearrange("p a k -> p (a k)"),
                                      xs[:, bass.ds(t, 1), :].rearrange("p a d -> p (a d)"))
                last.then_inc(st2_done, 1)

            def guards():
                g = mod[:, 2:6:3, :]
                dve.tensor_scalar(gneg[:], g, -1.0, None, ALU.mult).then_inc(g_chain, 1)
                dve.tensor_scalar(gsgn[:], g, 0.0, 2.0, ALU.is_ge, ALU.mult).then_inc(g_chain, 1)
                dve.wait_ge(g_chain, 2)
                dve.tensor_tensor(gabs[:], gneg[:], g, ALU.max).then_inc(g_chain, 1)
                dve.wait_ge(g_chain, 3)
                dve.tensor_scalar(gneg[:], gabs[:], 0.25, None, ALU.max).then_inc(g_chain, 1)
                dve.wait_ge(g_chain, 4)
                dve.scalar_tensor_tensor(out=gt[:], in0=gsgn[:], scalar=-1.0, in1=gneg[:], op0=ALU.add,
                                         op1=ALU.mult).then_inc(g_chain, 1)
                dve.wait_ge(g_chain, 5)
                dve.tensor_copy(gaB[:], gt[:, 0, :].unsqueeze(2).to_broadcast([P, NB, P])).then_inc(gaB_ready, 1)
                dve.wait_ge(small_in, 5 * DMA)
                dve.tensor_scalar(gbias[:], gb_t, sb2[:, 0:1], None, ALU.mult).then_inc(gb_ready, 1)
                dve.tensor_copy(gwh[:], gwT[:]).then_inc(gwsplit, 1)
                dve.wait_ge(gwsplit, 1)
                dve.tensor_tensor(gwl[:], gwT[:], gwh[:].bitcast(fp32), ALU.subtract).then_inc(gwsplit, 1)

            def replicated():
                dve.wait_ge(wsplit, 3)
                for n, w in enumerate((w4h, w4l)):
                    for c in range(3):
                        last = dve.tensor_copy(wrep[n][:, :, :, c, :],
                                               w[:, 0:2, :].bitcast(fp32).rearrange("p a (h d) -> p a h d", h=H))
                last.then_inc(wrep_done, 1)

            dve.wait_ge(cst_in, 3 * DMA)

            def body(b, par):
                for i in range(SLOTS):
                    if has(b, 1):
                        maximum(b + 1, 1 - par, i)
                    if i == 0 and has(b, 2):
                        normalise(b + 2)
                    if isinstance(b, int) and b == -2:
                        if i == 0:
                            replicated()
                        if i == 12:
                            stats1(range(FIRST, NT))
                            dve.wait_ge(st1_done, 2)
                            variances(1, range(FIRST, NT))
                    if isinstance(b, int) and b == -1:
                        if i == 1:
                            dve.wait_ge(std_done, 2)
                            dve.reciprocal(rstd1[:, FIRST:NT], std1[:, FIRST:NT]).then_inc(rstd_done, 1)
                            dve.wait_ge(rstd_done, 2)
                            guards()
                    if i == 2 and has(b, 0):
                        maxima_parts(b, 1)
                    if i == 3 and has(b, 2):
                        h_lo(b + 2, par)
                    if i in (4, 6) and has(b, -1):
                        divided(b - 1, (i - 4) // 2)
                    if i in (5, 7, 9, 11) and has(b, 2):
                        stacked(b + 2, (i - 5) // 2)
                    if i == 8 and has(b, -1):
                        concat_lo(b - 1)
                    if i == 10 and has(b, -1):
                        residual(b - 1)
                    if i == 11 and has(b, 1):
                        maxima_parts(b + 1, 0)
                    if i == 12 and has(b, -1):
                        stats2(b - 1)

            bodies(dve, body)
            divided(NB - 1, 0)
            divided(NB - 1, 1)
            concat_lo(NB - 1)
            residual(NB - 1)
            stats2(NB - 1)

            dve.wait_ge(st2_done, NB)
            for t in range(NT):
                last = dve.bn_aggr(mv2[:, t, :], st2[:, t, :])
            last.then_inc(mv2_done, 1)
            dve.wait_ge(mv2_done, 1)
            dve.tensor_scalar(std2[:], mv2[:, :, 1], EPS, None, ALU.add).then_inc(std2_in, 1)
            dve.wait_ge(std2_done, 1)
            dve.reciprocal(rstd2[:], std2[:]).then_inc(rstd2_done, 1)
            dve.wait_ge(rstd2_done, 1)

            def h2_lo(c):
                dve.wait_ge(h2_ready, 2 * c + 2)
                dve.tensor_tensor(H2l[:, c * CW:(c + 1) * CW], hf2[c % 2],
                                H2h[:, c * CW:(c + 1) * CW].bitcast(fp32), ALU.subtract).then_inc(h2l_ready, 1)

            for c in range(NC):
                if c >= 2:
                    dve.wait_ge(x2T_done, c - 1)
                for k in range(CT):
                    t = c * CT + k
                    last = dve.tensor_scalar(xn2[c % 2][:, k * P:(k + 1) * P], xs[:, t, :], mv2[:, t, 0:1],
                                           rstd2[:, t:t + 1], ALU.subtract, ALU.mult)
                last.then_inc(xn2_ready, 1)
                if c >= 1:
                    h2_lo(c - 1)
            h2_lo(NC - 1)

            step = [0]

            def link(ins):
                step[0] += 1
                ins.then_inc(route, 1)
                dve.wait_ge(route, step[0])

            def per_token(v):
                return v[:].unsqueeze(2).to_broadcast([P, NT, NE])

            def per_expert(v):
                return v[:].unsqueeze(1).to_broadcast([P, NT, NE])

            dve.wait_ge(gate_mm, 1)
            logits = bank[4][:, 0:NT * NE].rearrange("p (t n) -> p t n", t=NT)
            link(dve.tensor_reduce(out=r1[0][:], in_=logits, axis=AX.X, op=ALU.max))
            link(dve.tensor_tensor(lg[:], logits, per_token(r1[0]), ALU.subtract))
            dve.wait_ge(exp_gate, 1)
            link(dve.tensor_reduce(out=r1[1][:], in_=sc[:], axis=AX.X, op=ALU.add))
            link(dve.reciprocal(r1[2][:], r1[1][:]))
            link(dve.tensor_tensor(lg[:], sc[:], per_token(r1[2]), ALU.mult))
            link(dve.tensor_tensor(bi[:], lg[:], per_expert(gbb), ALU.add))
            for n in range(2):
                link(dve.tensor_reduce(out=r1[3 + 2 * n][:], in_=bi[:], axis=AX.X, op=ALU.max))
                link(dve.tensor_tensor(eq[:], bi[:], per_token(r1[3 + 2 * n]), ALU.is_ge))
                link(dve.tensor_tensor(cw[:], eq[:], per_expert(rev), ALU.mult))
                link(dve.tensor_reduce(out=r1[4 + 2 * n][:] if n == 0 else r1[0][:], in_=cw[:], axis=AX.X, op=ALU.max))
                link(dve.tensor_tensor(oh[n][:], cw[:], per_token(r1[4] if n == 0 else r1[0]), ALU.is_equal))
                if n == 0:
                    link(dve.scalar_tensor_tensor(out=bi[:], in0=oh[0][:], scalar=-3.0e38, in1=bi[:],
                                                op0=ALU.mult, op1=ALU.add))
            link(dve.tensor_tensor(eq[:], oh[0][:], oh[1][:], ALU.add))
            dve.tensor_tensor(cw[:], eq[:], lg[:], ALU.mult).then_inc(cw_done, 1)

            def chunk(c):
                for n in range(NX):
                    r = n % R
                    k = NX * c + n
                    dve.wait_ge(t1g_ready, k + 1)
                    if later(k - R + 1):
                        dve.wait_ge(sg_ready, k - R + 1)
                    if later(x_before(c, n)):
                        dve.wait_ge(x_ready, x_before(c, n))
                    dve.scalar_tensor_tensor(out=pg[r], in0=bank[2 * ((2 * n) % R) + 1][:], scalar=b13[:, n, 2:3],
                                           in1=t1g[r], op0=ALU.add, op1=ALU.mult).then_inc(pg_ready, 1)
                    dve.wait_ge(pg_ready, k + 1)
                    dve.tensor_scalar(pg[r], pg[r], LIMIT, None, ALU.min).then_inc(gm_ready, 1)
                    if n > 0 or not isinstance(c, int):
                        weighted(c, n - 1) if n > 0 else weighted(c - 1, NX - 1)
                    dve.wait_ge(t1l_ready, k + 1)
                    dve.scalar_tensor_tensor(out=pl[r], in0=bank[2 * ((2 * n + 1) % R) + 1][:], scalar=b13[:, n, 3:4],
                                           in1=t1l[r], op0=ALU.add, op1=ALU.mult).then_inc(pl_ready, 1)
                    dve.wait_ge(pl_ready, k + 1)
                    dve.tensor_scalar(pl[r], pl[r], -LIMIT, LIMIT, ALU.max, ALU.min).then_inc(lc_ready, 1)
                    if n == 4 and not isinstance(c, int):
                        finish(c - 1)

            def weighted(c, n):
                r = n % R
                k = NX * c + n
                dve.wait_ge(lc_ready, k + 1)
                if n > 0:
                    dve.wait_ge(x_ready, NE * c + n)
                else:
                    if later(k - R + 1):
                        dve.wait_ge(a_ready, k - R + 1)
                dve.scalar_tensor_tensor(out=X[r], in0=pl[r], scalar=1.0, in1=X[r] if n > 0 else pg[r],
                                       op0=ALU.add, op1=ALU.mult).then_inc(yx_ready, 1)

            def finish(c):
                dve.wait_ge(zT_done, c + 1)
                dve.wait_ge(dram_out, DMA * (c + 1))
                dve.tensor_tensor(yo, bank[Z_BANK][:].rearrange("p (t d) -> p t d", t=CT),
                                xs[:, bass.ds(c * CT, CT), :], ALU.add).then_inc(yo_ready, 1)

            chunk(0)
            with dve.Fori(1, NC) as c:
                chunk(c)
            weighted(NC - 1, NX - 1)
            finish(NC - 1)

        @block.tensor
        def _(pe):
            def product(out, hi, lo, rhi, rlo):
                pe.matmul(out, hi, rhi, start=True, stop=False)
                pe.matmul(out, lo, rhi, start=False, stop=False)
                return pe.matmul(out, hi, rlo, start=False, stop=True)

            pe.wait_ge(silu_done, 1)
            pe.wait_ge(c_in, 2 * DMA)
            for k in range(6):
                last = pe.matmul(bank[0][:, k * NB:(k + 1) * NB], wmod[:, k, :], siluT[:], start=True, stop=True)
            last.then_inc(mod_mm, 1)

            def normedT(b):
                pe.wait_ge(xn_ready, b + 1)
                if later(b - 1):
                    pe.wait_ge(v_ready, b - 1)
                if isinstance(b, int) and b == 1:
                    pe.wait_ge(stage_ready, 4)
                for k in range(TB):
                    last = pe.transpose(bank[A_BANK][:, k * P:(k + 1) * P], xn[:, k, :], ident[:])
                last.then_inc(xnT_done, 1)

            def qk_step(b, par, n):
                pe.wait_ge(hl_ready, b + 1)
                if later(4 * b + n) and not (isinstance(b, int) and b == 0):
                    pe.wait_ge(stage_ready, 4 * b + n)
                qk, half = n // 2, n % 2
                for k in range(2):
                    g = 2 * half + k
                    wh = wrep[0][:, qk, J * g:J * g + J].rearrange("p h c d -> p (h c d)")
                    wl = wrep[1][:, qk, J * g:J * g + J].rearrange("p h c d -> p (h c d)")
                    last = product(a_bank(b, n)[:, k * S:(k + 1) * S], wh, wl, hh[par][:], hl[par][:])
                last.then_inc(qk_mm, 1)

            def values(b, par):
                last_row = isinstance(b, int) and b == NB - 1
                pe.wait_ge(stage_ready, 4 * (b + 1 if last_row else b + 2))
                for k in range(TB):
                    tk = slice(k * P, (k + 1) * P)
                    last = product(bank[A_BANK][:, k * D:(k + 1) * D], hh[par][:, tk], hl[par][:, tk],
                                   w4h[:, 2, :], w4l[:, 2, :])
                last.then_inc(v_mm, 1)

            def scores_q(b, par, i):
                u = SLOTS * b + i
                pair, qt = i // 2, i % 2
                g = pair // 2
                if i % 4 == 0:
                    pe.wait_ge(copied, G * b + g + 1)
                if later(u - 1):
                    pe.wait_ge(max_done, u - 1)
                pe.matmul(bank[S_BANK + i % 2][:], Qst[par][:, g, qt * P:(qt + 1) * P],
                         Kx[:, par, 2 * pair:2 * pair + 2, :].rearrange("p a b -> p (a b)"),
                         start=True, stop=True).then_inc(s_mm, 1)

            def scores_k(b, par, h):
                u = SLOTS * b + h
                if h % (H // 2) == 0:
                    pe.wait_ge(mrow[h // (H // 2)], 4 * DMA * (b + 1))
                if later(u - 1):
                    pe.wait_ge(exp_done, u - 1)
                for k in range(TB):
                    last = pe.matmul(bank[ST_BANK + h % 2][:, k * S:(k + 1) * S], Kx[:, par, h, k * P:(k + 1) * P],
                                    Qst[par][:, h // J, :], start=True, stop=True)
                last.then_inc(st_mm, 1)

            def attend(b, par, g):
                pe.wait_ge(exp_done, SLOTS * b + J * g + J)
                pe.wait_ge(v_ready, b + 1)
                if later(G * b + g - 1):
                    pe.wait_ge(ot_ready, G * b + g - 1)
                for k in range(TB):
                    for j in range(J):
                        h = J * g + j
                        last = pe.matmul(bank[PV_BANK][32 * j:32 * j + 32, (g % 2) * S:(g % 2 + 1) * S],
                                        V[par][:, k, h, :], pt[h % PE_RING][:, k * S:(k + 1) * S],
                                        start=k == 0, stop=k == TB - 1, skip_group_check=True)
                last.then_inc(pv_mm, 1)

            def maximaT(b, par, half):
                pe.wait_ge(max_done, SLOTS * b + 8 * half + 8)
                if half == 1:
                    pe.wait_ge(m_split, 4 * b + 2)
                elif not (isinstance(b, int) and b == 0):
                    pe.wait_ge(m_split, 4 * b)
                    if later(b - 1):
                        pe.wait_ge(ccl_ready, b - 1)
                for k in range(TB):
                    last = pe.transpose(bank[T_BANK][0:8, k * P:(k + 1) * P],
                                       M[:, par, k, 8 * half:8 * half + 8], ident[:])
                last.then_inc(mT_done, 1)

            def attendedT(b, qt):
                pe.wait_ge(ot_ready, G * b + G)
                if later(b):
                    pe.wait_ge(rt_ready, b)
                if later(TB * b + qt):
                    pe.wait_ge(cc_ready, TB * b + qt)
                if isinstance(b, int) and b == 0:
                    pe.wait_ge(ga_ready, 2)
                for g in range(G):
                    last = pe.transpose(bank[O_BANK][:, g * P:(g + 1) * P], OT[:, g, qt * P:(qt + 1) * P], ident[:])
                last.then_inc(otr_mm, 1)

            def concatT(b):
                pe.wait_ge(cc_ready, TB * b + TB)
                if later(b):
                    pe.wait_ge(ccl_ready, b)
                if isinstance(b, int) and b == NB - 1:
                    pe.wait_ge(m_split, 4 * NB)
                else:
                    pe.wait_ge(m_split, 4 * (b + 2))
                for k in range(TB):
                    last = pe.transpose(bank[T_BANK][:, k * P:(k + 1) * P], cc[:, k, :], ident[:])
                last.then_inc(cT_mm, 1)

            def output(b):
                pe.wait_ge(ccl_ready, b + 1)
                for k in range(TB):
                    tk = slice(k * P, (k + 1) * P)
                    last = product(bank[O_BANK][:, k * D:(k + 1) * D], cch[:, tk], ccl[:, tk],
                                   w4h[:, 3, :], w4l[:, 3, :])
                last.then_inc(o_mm, 1)

            pe.wait_ge(cst_in, 3 * DMA)

            def body(b, par):
                for i in range(SLOTS):
                    if has(b, 1):
                        scores_q(b + 1, 1 - par, i)
                    if has(b, 0):
                        scores_k(b, par, i)
                    if i == 1 and has(b, -1):
                        attend(b - 1, 1 - par, G - 1)
                    if i == 1 and has(b, 0):
                        maximaT(b, par, 1)
                    if i == 4 and isinstance(b, int) and b == -2:
                        pe.wait_ge(wrep_done, 1)
                    if i == 4 and isinstance(b, int) and b == -1:
                        pe.wait_ge(gaB_ready, 1)
                        for k in range(NB):
                            last = pe.matmul(bank[ST_BANK + k // 4][:, (k % 4) * D:(k % 4 + 1) * D], gaB[:, k, :],
                                             ident[:], start=True, stop=True)
                        last.then_inc(ga_mm, 1)
                    if i == 1 and has(b, 2):
                        normedT(b + 2)
                    if i in (3, 5) and has(b, -1):
                        attendedT(b - 1, (i - 3) // 2)
                    if i in (4, 6, 8, 10) and has(b, 2):
                        qk_step(b + 2, par, (i - 4) // 2)
                    if i in (5, 9, 13) and has(b, 0):
                        attend(b, par, (i - 5) // 4)
                    if i == 7 and has(b, -1):
                        concatT(b - 1)
                    if i == 9 and has(b, -1):
                        output(b - 1)
                    if i == 10 and has(b, 1):
                        maximaT(b + 1, 1 - par, 0)
                    if i == 12 and has(b, 1):
                        values(b + 1, 1 - par)

            bodies(pe, body)
            attend(NB - 1, (NB - 1) % 2, G - 1)
            attendedT(NB - 1, 0)
            attendedT(NB - 1, 1)
            concatT(NB - 1)
            output(NB - 1)

            def gate(c):
                pe.wait_ge(h2l_ready, c + 1)
                for k in range(CT):
                    t = c * CT + k
                    tk = slice(t * P, (t + 1) * P)
                    last = product(bank[4][:, t * NE:(t + 1) * NE], H2h[:, tk], H2l[:, tk], gwh[:], gwl[:])
                if c == NC - 1:
                    last.then_inc(gate_mm, 1)

            pe.wait_ge(gwsplit, 2)
            for c in range(NC):
                pe.wait_ge(xn2_ready, c + 1)
                if c >= 2:
                    pe.wait_ge(h2_ready, 2 * (c - 1))
                for k in range(CT):
                    last = pe.transpose(bank[c % 2][:, k * P:(k + 1) * P], xn2[c % 2][:, k * P:(k + 1) * P], ident[:])
                last.then_inc(x2T_done, 1)
                if c >= 1:
                    gate(c - 1)
            gate(NC - 1)
            pe.wait_ge(cw_done, 1)
            for c in range(NC):
                for k in range(CT):
                    last = pe.transpose(bank[c][0:NE, k * P:(k + 1) * P], cw[:, c * CT + k, :], ident[:])
                last.then_inc(cwT_mm, 1)

            def first_layer(c, n):
                rhi, rlo = H2h[:, bass.ds(c * CW, CW)], H2l[:, bass.ds(c * CW, CW)]
                for part, done in ((0, g_mm), (1, l_mm)):
                    u = 2 * n + part
                    prev = u - R
                    k = NX * c + prev // 2
                    if later(k + 1) and prev % 2:
                        pe.wait_ge(pl_ready, k + 1)
                    elif later(k + 1):
                        pe.wait_ge(pg_ready, k + 1)
                    for m in range(2):
                        w = slice((2 * m + part) * P, (2 * m + part + 1) * P)
                        last = product(bank[2 * (u % R) + m][:], w13h[:, n, w], w13l[:, n, w], rhi, rlo)
                    last.then_inc(done, 1)

            def second_layer(c, n):
                pe.wait_ge(a_ready, NX * c + n + 1)
                if n == 0:
                    if later(c):
                        pe.wait_ge(z_ready, c)
                pe.matmul(bank[Y_BANK][:], w2[:, n, :], av[n % R], start=n == 0, stop=False).then_inc(w2_mm, 1)
                if n == NX - 1:
                    pe.matmul(bank[Y_BANK][:], b2[:], cwT[:, bass.ds(c * CW, CW)], start=False, stop=True)\
                     .then_inc(y_ready, 1)

            def backT(c):
                pe.wait_ge(z_ready, c + 1)
                for k in range(CT):
                    last = pe.transpose(bank[Z_BANK][:, k * P:(k + 1) * P], zb[:, k * P:(k + 1) * P], ident[:])
                last.then_inc(zT_done, 1)

            LAG = 2

            def chunk(c):
                for n in range(NX):
                    first_layer(c, n)
                    if n >= LAG:
                        second_layer(c, n - LAG)
                    elif not isinstance(c, int):
                        second_layer(c - 1, NX + n - LAG)
                    if n == 3 and not isinstance(c, int):
                        backT(c - 1)

            pe.wait_ge(w13lo, NX)
            pe.wait_ge(w2_in, DMA)
            pe.wait_ge(small_in, 5 * DMA)
            pe.wait_ge(cwT_done, NC)
            chunk(0)
            with pe.Fori(1, NC) as c:
                chunk(c)
            for n in range(NX - LAG, NX):
                second_layer(NC - 1, n)
            backT(NC - 1)


def kernel(**inputs):
    import numpy as np
    import concourse.bacc as _bacc
    from concourse import mybir as _mybir
    from concourse.bass_utils import run_bass_kernel_spmd as _run

    a = {k: np.asarray(v) for k, v in inputs.items()}
    x = a["L0_attn_x"]
    B, S, D = x.shape
    P = 128
    NT = B * S // P
    x_l = x.reshape(NT, P, D).transpose(1, 0, 2)
    w4 = np.stack([a["L0_attn_w_" + n].T for n in "qkvo"], axis=1)
    E, F2, _ = a["L0_ffn_w1"].shape
    w1 = np.concatenate([a["L0_ffn_sw1"][None], a["L0_ffn_w1"]])
    w3 = np.concatenate([a["L0_ffn_sw3"][None], a["L0_ffn_w3"]])
    w13 = np.concatenate([w1[:, 0::2], w1[:, 1::2], w3[:, 0::2], w3[:, 1::2]], axis=1).transpose(2, 0, 1)
    b1 = np.concatenate([a["L0_ffn_sb1"][None], a["L0_ffn_b1"]])
    b3 = np.concatenate([a["L0_ffn_sb3"][None], a["L0_ffn_b3"]])
    b13 = np.stack([b1[:, 0::2], b1[:, 1::2], b3[:, 0::2], b3[:, 1::2]], axis=1).transpose(2, 0, 1)
    w2 = np.concatenate([a["L0_ffn_sw2"][None], a["L0_ffn_w2"]]).transpose(2, 0, 1)
    row = np.arange(P) % 32
    c = row // 8
    one = row // 2 == 12
    cols = np.stack([np.where(c == 1, -1.0, 0.0), np.where(c == 2, -1.0, np.where(one, 1.0, 0.0)),
                     np.where(one, 1.0, 0.0)] + [np.where(np.arange(P) // 32 == j, 1.0, 0.0) for j in range(4)],
                    axis=1).astype(np.float32)
    ins = {
        "x": x_l, "w4": w4, "cT": a["L0_c"].T, "wmod": a["L0_wmod"].reshape(D, 6, D), "w13": w13, "w2": w2,
        "b13": b13, "b2": a["L0_ffn_b2"], "sb2": a["L0_ffn_sb2"].reshape(D, 1), "gw": a["L0_ffn_gate_w"].T,
        "gb": a["L0_ffn_gate_b"], "ident": np.eye(P, dtype=np.float32), "cols": cols,
        "rev": np.ascontiguousarray(np.broadcast_to(np.arange(E, 0, -1, dtype=np.float32), (P, E))),
    }
    nc = _bacc.Bacc("TRN2", target_bir_lowering=False, num_devices=1)
    arrays, args = {}, []
    for name, v in ins.items():
        v = np.ascontiguousarray(v)
        arrays[f"in_{name}"] = v
        args.append(nc.dram_tensor(f"in_{name}", v.shape, _mybir.dt.from_np(v.dtype), kind="ExternalInput").ap())
    args.append(nc.dram_tensor("out_y", (P, NT, D), _mybir.dt.float32, kind="ExternalOutput").ap())
    block_kernel(nc, *args)
    r = _run(nc, [arrays], core_ids=[0])
    y = r.results[0]["out_y"]
    return y.transpose(1, 0, 2).reshape(B, S, D)
```

```python
from contextlib import ExitStack

import concourse.bass as bass
from concourse import mybir


def block_kernel(nc, x_d, w4_d, cT_d, wmod_d, w13_d, w2_d, b13_d, b2_d, sb2_d, gw_d, gb_d, ident_d, cols_d, rev_d, y_d):
    fp32, f32r = mybir.dt.float32, mybir.dt.float32r
    ALU, ACT, AX = mybir.AluOpType, mybir.ActivationFunctionType, mybir.AxisListType
    P = 128
    D = x_d.shape[2]
    NT = x_d.shape[1]
    NB = cT_d.shape[1]
    TB = NT // NB
    S = TB * P
    HD = 8
    H = D // HD
    G = 4
    J = H // G
    SCALE = float(HD) ** -0.5
    EPS = 1e-5
    NE = gw_d.shape[1]
    NX = NE + 1
    CT = 4
    CW = CT * P
    NC = NT // CT
    ALPHA, LIMIT = 1.702, 7.0
    SLOTS = H
    QK_AT, STACK_AT = (5, 8, 11, 14), (6, 9, 12, 15)
    XNT_AT, H_AT, HL_AT = 2, 2, 3
    V_AT, V_OUT_AT = 11, 11
    ATTEND_AT, ATTEND_OUT_AT = (5, 9, 13), (6, 10, 14)
    MAXT1_AT, PARTS1_AT = 1, 1
    MAXT0_AT, PARTS0_AT = 9, 9
    OT_AT, DIV_AT = (5, 8), (5, 8)
    CT_AT, CHI_AT, CLO_AT = 12, 12, 13
    OUT_AT, RES_AT, ST2_AT = 15, 15, 15
    DMA = 16

    cwd = nc.dram_tensor("cw_scratch", (NE, NT * P), fp32, kind="Internal").ap()

    ctx = ExitStack()
    with ctx:
        def sb(name, shape, dt=fp32):
            return ctx.enter_context(nc.sbuf_tensor(name, shape, dt))

        def sem(name):
            return ctx.enter_context(nc.semaphore(name))

        xs = sb("xs", [P, NT, D])
        w4 = sb("w4", [P, 4, P])
        w4h = sb("w4h", [P, 4, P], f32r)
        w4l = sb("w4l", [P, 4, P], f32r)
        wrep = [sb(f"wrep{n}", [P, 2, H, 4, HD], f32r) for n in range(2)]
        cT = sb("cT", [P, NB])
        sigc = sb("sigc", [P, NB])
        siluT = sb("siluT", [P, NB])
        gaB = sb("gaB", [P, NB, P])
        mod = sb("mod", [P, 6, NB])
        mod1 = sb("mod1", [P, 6, NB])
        gneg = sb("gneg", [P, 2, NB])
        gabs = sb("gabs", [P, 2, NB])
        gsgn = sb("gsgn", [P, 2, NB])
        gt = sb("gt", [P, 2, NB])
        gb_t = gt[:, 1, :]
        gbias = sb("gbias", [P, NB])
        ga_b = sb("ga_b", [P, NB, D])
        st1 = sb("st1", [P, NT, 6])
        mv1 = sb("mv1", [P, NT, 2])
        std1 = sb("std1", [P, NT])
        rstd1 = sb("rstd1", [P, NT])
        ident = sb("ident", [P, P])
        cols = sb("cols", [P, 3 + J])
        rev = sb("rev", [P, NE])
        zcol = sb("zcol", [P, 1])
        xn = sb("xn", [P, TB, D])
        hf = sb("hf", [P, S])
        hh = [sb(f"hh{n}", [P, S], f32r) for n in range(2)]
        hl = [sb(f"hl{n}", [P, S], f32r) for n in range(2)]
        hiS = [sb(f"hiS{n}", [P, 2, S], f32r) for n in range(2)]
        stage = sb("stage", [P, 2, G, S], f32r)
        Qst = [sb(f"Qst{n}", [P, G, S], f32r) for n in range(2)]
        Kx = sb("Kx", [P, 2, H, S], f32r)
        Vb = sb("Vb", [P, 2, TB, H, 32])
        V = [Vb[:, n] for n in range(2)]
        M = sb("M", [P, 2, TB, H])
        mhl = sb("mhl", [8, 2, 2, S], f32r)
        OT = sb("OT", [P, G, S])
        rd = sb("rd", [P, TB, H])
        cc = sb("cc", [P, TB, D])
        cch = sb("cch", [P, S], f32r)
        ccl = sb("ccl", [P, S], f32r)
        rt = sb("rt", [P, TB, D])
        st2 = sb("st2", [P, NT, 6])
        mv2 = sb("mv2", [P, NT, 2])
        std2 = sb("std2", [P, NT])
        rstd2 = sb("rstd2", [P, NT])
        w13h = sb("w13h", [P, NX, 4 * P], f32r)
        w13l = sb("w13l", [P, NX, 4 * P], f32r)
        w2 = sb("w2", [P, NX, P])
        b13 = sb("b13", [P, NX, 4])
        b2 = sb("b2", [P, D])
        sb2 = sb("sb2", [P, 1])
        gwT = sb("gwT", [P, NE])
        gwh = sb("gwh", [P, NE], f32r)
        gwl = sb("gwl", [P, NE], f32r)
        gbb = sb("gbb", [P, NE])
        NF = 21
        F = sb("F", [P, NF, CW])
        w13 = F[:, 0:NX, :]
        PE_RING = 8
        pt = [F[:, NX + n, :] for n in range(PE_RING)]
        R = 3
        t1g, t1l, pg, pl, X, sg, av = [[F[:, R * k + n, :] for n in range(R)] for k in range(7)]
        cwB = sb("cwB", [P, R, CW])
        H2h = Kx[:, 0, 0:H // 2, :].rearrange("p a b -> p (a b)")
        H2l = Kx[:, 0, H // 2:H, :].rearrange("p a b -> p (a b)")
        wmod = F[:, NX + PE_RING + 2:NX + PE_RING + 4, :].rearrange("p a b -> p (a b)")[:, 0:6 * D]\
            .rearrange("p (a b) -> p a b", a=6)
        cwT = stage[:].bitcast(fp32).rearrange("p a g s -> p (a g s)")
        xn2 = [hiS[n][:].bitcast(fp32).rearrange("p a b -> p (a b)") for n in range(2)]
        hf2 = [gaB[:, 0:4, :].rearrange("p a b -> p (a b)"), gaB[:, 4:8, :].rearrange("p a b -> p (a b)")]
        zb = ga_b[:, 0:4, :].rearrange("p a b -> p (a b)")
        yo = ga_b[:, 4:8, :]
        lg = sb("lg", [P, NT, NE])
        sc = sb("sc", [P, NT, NE])
        bi = sb("bi", [P, NT, NE])
        eq = sb("eq", [P, NT, NE])
        oh = [sb(f"oh{n}", [P, NT, NE]) for n in range(2)]
        cw = sb("cw", [P, NT, NE])
        r1 = [sb(f"r1_{n}", [P, NT]) for n in range(7)]

        bank = [ctx.enter_context(nc.psum_tensor(f"bank{n}", [P, 512], fp32)) for n in range(8)]
        S_BANK, ST_BANK, PV_BANK, A_BANK, O_BANK, T_BANK = 0, 2, 4, 5, 6, 7
        Y_BANK, Z_BANK = 6, 7
        GATE_BANK = (A_BANK, T_BANK)
        half_bank = bank[O_BANK][:, 0:S]

        x_in = [sem(f"x_in{n}") for n in range(4)]
        c_in = sem("c_in")
        w4_in = sem("w4_in")
        cst_in = sem("cst_in")
        w13_in = sem("w13_in")
        small_in = sem("small_in")
        w2_in = sem("w2_in")
        dram_out = sem("dram_out")
        cw_late_out = sem("cw_late_out")
        idle_zero = sem("idle_zero")
        b2_zero = sem("b2_zero")
        wsplit = sem("wsplit")
        wrep_done = sem("wrep_done")
        silu_sig = sem("silu_sig")
        silu_done = sem("silu_done")
        mod_mm = sem("mod_mm")
        mod_done = sem("mod_done")
        ga_mm = sem("ga_mm")
        g_chain = sem("g_chain")
        gaB_ready = sem("gaB_ready")
        ga_ready = sem("ga_ready")
        gb_ready = sem("gb_ready")
        gwsplit = sem("gwsplit")
        w13hi = sem("w13hi")
        w13lo = sem("w13lo")
        st1_done = sem("st1_done")
        mv1_done = sem("mv1_done")
        std_in = sem("std_in")
        std_done = sem("std_done")
        rstd_done = sem("rstd_done")
        xn_ready = sem("xn_ready")
        xnT_done = sem("xnT_done")
        h_ready = sem("h_ready")
        hl_ready = sem("hl_ready")
        qk_mm = sem("qk_mm")
        hi_ready = sem("hi_ready")
        stage_ready = sem("stage_ready")
        copied = sem("copied")
        s_mm = sem("s_mm")
        max_done = sem("max_done")
        mT_done = sem("mT_done")
        m_split = sem("m_split")
        mrow = [sem(f"mrow{n}") for n in range(2)]
        st_mm = sem("st_mm")
        exp_done = sem("exp_done")
        v_mm = sem("v_mm")
        v_ready = sem("v_ready")
        pv_mm = sem("pv_mm")
        ot_ready = sem("ot_ready")
        otr_mm = sem("otr_mm")
        rd_ready = sem("rd_ready")
        cc_ready = sem("cc_ready")
        cT_mm = sem("cT_mm")
        cch_ready = sem("cch_ready")
        ccl_ready = sem("ccl_ready")
        o_mm = sem("o_mm")
        rt_ready = sem("rt_ready")
        x2_ready = sem("x2_ready")
        st2_done = sem("st2_done")
        mv2_done = sem("mv2_done")
        std2_in = sem("std2_in")
        std2_done = sem("std2_done")
        rstd2_done = sem("rstd2_done")
        xn2_ready = sem("xn2_ready")
        x2T_done = sem("x2T_done")
        h2_ready = sem("h2_ready")
        h2l_ready = sem("h2l_ready")
        gate_mm = sem("gate_mm")
        lg_ready = sem("lg_ready")
        route = sem("route")
        exp_gate = sem("exp_gate")
        cw_done = sem("cw_done")
        cwT_zero = sem("cwT_zero")
        cwT_mm = sem("cwT_mm")
        cwT_done = sem("cwT_done")
        cwB_in = [sem(f"cwB_in{n}") for n in range(R)]
        g_mm = sem("g_mm")
        l_mm = sem("l_mm")
        t1g_ready = sem("t1g_ready")
        t1l_ready = sem("t1l_ready")
        pg_ready = sem("pg_ready")
        gm_ready = sem("gm_ready")
        pl_ready = sem("pl_ready")
        lc_ready = sem("lc_ready")
        sg_ready = sem("sg_ready")
        x_ready = sem("x_ready")
        yx_ready = sem("yx_ready")
        a_ready = sem("a_ready")
        w2_mm = sem("w2_mm")
        y_ready = sem("y_ready")
        z_ready = sem("z_ready")
        zT_done = sem("zT_done")
        yo_ready = sem("yo_ready")

        PE_X2T, PE_GATE = (1, 3, 5), (6, 8, 10)
        DVE_XN2, DVE_H2L = (1, 2, 3), (4, 6, 8)
        ACT_H2 = (2, 4, 6)

        def x2_bank(c):
            return S_BANK + c % 2 if c < EARLY else T_BANK

        def later(value):
            return not isinstance(value, int) or value > 0

        block = ctx.enter_context(nc.Block())

        def x_before(c, n):
            return NE * c + (n - R if n >= R else n - R + 1)

        def bodies(e, body):
            for b in range(-2, 2):
                body(b, b % 2)
            with e.Fori(0, (NB - 4) // 2) as i:
                body(2 * i + 2, 0)
                body(2 * i + 3, 1)
            for b in range(NB - 2, NB):
                body(b, b % 2)

        def has(b, stage_of):
            return not isinstance(b, int) or 0 <= b + stage_of < NB

        def a_bank(b, n):
            return bank[(A_BANK, PV_BANK, O_BANK, T_BANK)[n] if isinstance(b, int) and b == 0 else A_BANK]

        def o_bank(b, qt):
            return T_BANK if isinstance(b, int) and b == NB - 1 and qt == 1 else O_BANK

        def out_psum(b):
            if isinstance(b, int) and b == NB - 1:
                return bank[T_BANK][:, TB * P:TB * P + TB * D]
            return bank[O_BANK][:, 0:TB * D]

        FIRST = 4
        EARLY = NC - 1
        part_tiles = [slice(0, EARLY * CT), slice(EARLY * CT, NT)]
        CWT_BANK = (A_BANK, O_BANK, T_BANK, T_BANK)

        @block.sync
        def _(sp):
            sp.dma_start(cT[:], cT_d).then_inc(c_in, DMA)
            q = NT // 4
            for n in range(4):
                sp.dma_start(xs[:, n * q:(n + 1) * q, :], x_d[:, n * q:(n + 1) * q, :]).then_inc(x_in[n], DMA)
                if n == 0:
                    sp.dma_start(wmod, wmod_d).then_inc(c_in, DMA)
                    sp.dma_start(w4[:], w4_d).then_inc(w4_in, DMA)
                    for dst, src in ((ident, ident_d), (cols, cols_d), (rev, rev_d)):
                        sp.dma_start(dst[:], src).then_inc(cst_in, DMA)
            sp.wait_ge(b2_zero, 1)
            sp.dma_start(b2[0:NE, :], b2_d).then_inc(small_in, DMA)
            sp.dma_start(sb2[:], sb2_d).then_inc(small_in, DMA)
            sp.dma_start(gwT[:], gw_d).then_inc(small_in, DMA)
            sp.dma_start(gbb[:], gb_d.partition_broadcast(P)).then_inc(small_in, DMA)
            sp.dma_start(b13[:], b13_d).then_inc(small_in, DMA)
            sp.dma_start(w13, w13_d).then_inc(w13_in, DMA)
            sp.dma_start(w2[:], w2_d).then_inc(w2_in, DMA)

            def maxima_rows(b, par, half):
                sp.wait_ge(m_split, 4 * b + 2 * half + 2)
                for part in range(2):
                    for g2 in range(2):
                        sp.dma_start(Qst[par][24 + part:P:32, 2 * half + g2, :].bitcast(fp32),
                                    mhl[J * g2:J * g2 + J, half, part, :].bitcast(fp32)).then_inc(mrow[half], DMA)

            def body(b, par):
                if has(b, 0):
                    maxima_rows(b, par, 1)
                if has(b, 1):
                    maxima_rows(b + 1, 1 - par, 0)

            bodies(sp, body)

            sp.wait_ge(cwT_done, EARLY)
            sp.dma_start(cwd[:, 0:EARLY * CW], cwT[0:NE, 0:EARLY * CW]).then_inc(dram_out, DMA)
            sp.wait_ge(dram_out, DMA)

            def chunk(c):
                for n in range(1, NX):
                    r = n % R
                    if later(x_before(c, n)):
                        sp.wait_ge(x_ready, x_before(c, n))
                    sp.dma_start(cwB[:, r, :], cwd[n - 1, bass.ds(c * CW, CW)].partition_broadcast(P))\
                     .then_inc(cwB_in[r], DMA)

            def store(c):
                sp.wait_ge(yo_ready, c + 1)
                sp.dma_start(y_d[:, bass.ds(c * CT, CT), :], yo).then_inc(dram_out, DMA)

            chunk(0)
            with sp.Fori(1, NC) as c:
                chunk(c)
                sp.wait_ge(cw_late_out, DMA)
                store(c - 1)
            store(NC - 1)
            sp.wait_ge(dram_out, (NC + 1) * DMA)

        @block.gpsimd
        def _(pool):
            pool.memset(zcol[:], 0.0)
            for n in range(2):
                pool.memset(V[n], 0.0).then_inc(idle_zero, 1)
            pool.wait_ge(idle_zero, 2)
            for n in range(2):
                pool.memset(V[n][:, :, :, HD:HD + 1], 1.0).then_inc(idle_zero, 1)
            pool.memset(b2[:], 0.0).then_inc(b2_zero, 1)

            def split_w13(n):
                pool.wait_ge(w13_in, DMA)
                pool.tensor_scalar(w13h[:, n, :], w13[:, n, :], 1.0, 0.0, ALU.mult, ALU.add).then_inc(w13hi, 1)
                pool.wait_ge(w13hi, n + 1)
                pool.tensor_tensor(w13l[:, n, :], w13[:, n, :], w13h[:, n, :].bitcast(fp32), ALU.subtract)\
                 .then_inc(w13lo, 1)

            def copy_group(b, par, g, reuse):
                pool.wait_ge(stage_ready, 4 * b + (2 if g < 2 else 4))
                if reuse:
                    pool.wait_ge(st_mm, SLOTS * (b - 2) + J * g + J)
                pool.tensor_tensor(Qst[par][:, g, :], stage[:, 0, g, :].bitcast(fp32), zcol[:].to_broadcast([P, S]),
                                ALU.add)
                for j in range(J):
                    last = pool.tensor_scalar(Kx[:, par, J * g + j, :], stage[:, 1, g, :].bitcast(fp32),
                                           cols[:, 3 + j:4 + j], 0.0, ALU.mult, ALU.add)
                last.then_inc(copied, 1)

            pool.wait_ge(cst_in, 3 * DMA)

            def body(b, par):
                if has(b, 2):
                    for g in range(G):
                        copy_group(b + 2, par, g, has(b, 0))
                if isinstance(b, int) and b == NB - 2:
                    pool.wait_ge(copied, G * NB)
                    pool.memset(cwT, 0.0).then_inc(cwT_zero, 1)
                if isinstance(b, int):
                    for n in {-2: (0, 1), -1: (2,), 0: (3,), 1: (4,), NB - 2: (5, 6), NB - 1: (7, 8)}[b]:
                        split_w13(n)

            bodies(pool, body)
            pool.wait_ge(pv_mm, G * NB)

            def expert(c, n):
                r = n % R
                k = NX * c + n
                if n > 0:
                    pool.wait_ge(gm_ready, k + 1)
                    pool.wait_ge(cwB_in[r], DMA * (len(range(r or R, NX, R)) * c + len(range(r or R, n + 1, R))))
                    if later(k - R + 1):
                        pool.wait_ge(a_ready, k - R + 1)
                    pool.tensor_tensor(X[r], pg[r], cwB[:, r, :], ALU.mult).then_inc(x_ready, 1)

            def gate(c, n):
                r = n % R
                k = NX * c + n
                pool.wait_ge(yx_ready, k + 1)
                pool.wait_ge(sg_ready, k + 1)
                if later(k - R + 1):
                    pool.wait_ge(w2_mm, k - R + 1)
                pool.tensor_tensor(av[r], X[r], sg[r], ALU.mult).then_inc(a_ready, 1)

            def chunk(c):
                for n in range(NX):
                    expert(c, n)
                    if n > 0 or not (isinstance(c, int) and c == 0):
                        k = NX * c + n - 1
                        gate(c, n - 1) if n > 0 else gate(c - 1, NX - 1)

            chunk(0)
            with pool.Fori(1, NC) as c:
                chunk(c)
            gate(NC - 1, NX - 1)

        @block.scalar
        def _(act):
            act.wait_ge(c_in, 2 * DMA)
            act.activation(sigc[:], cT[:], ACT.Sigmoid).then_inc(silu_sig, 1)
            act.wait_ge(mod_mm, 1)
            act.activation(mod[:], bank[0][:, 0:6 * NB].rearrange("p (a b) -> p a b", a=6), ACT.Identity)\
             .then_inc(mod_done, 1)
            act.wait_ge(std_in, 1)
            act.activation(std1[:, 0:FIRST], std1[:, 0:FIRST], ACT.Sqrt).then_inc(std_done, 1)

            def normed(b, par):
                act.wait_ge(xnT_done, b + 1)
                if later(b):
                    act.wait_ge(hl_ready, b)
                src = half_bank
                act.activation(hf[:], src, ACT.Identity, bias=mod[:, 0, bass.ds(b, 1)],
                             scale=mod1[:, 1, bass.ds(b, 1)]).then_inc(h_ready, 1)
                act.activation(hh[par][:], src, ACT.Identity, bias=mod[:, 0, bass.ds(b, 1)],
                             scale=mod1[:, 1, bass.ds(b, 1)]).then_inc(h_ready, 1)

            def hi_part(b, n):
                act.wait_ge(qk_mm, 4 * b + n + 1)
                if later(4 * b + n - 1):
                    act.wait_ge(stage_ready, 4 * b + n - 1)
                act.activation(hiS[n % 2][:], a_bank(b, n)[:].rearrange("p (a b) -> p a b", a=2), ACT.Identity,
                             bias=cols[:, 2:3] if n % 2 == 1 else 0.0).then_inc(hi_ready, 1)

            def values(b, par):
                act.wait_ge(v_mm, b + 1)
                if later(G * (b - 1)):
                    act.wait_ge(pv_mm, G * (b - 1))
                act.activation(V[par][:, :, :, 0:HD],
                             half_bank.rearrange("p (t h d) -> p t h d", t=TB, h=H), ACT.Identity)\
                 .then_inc(v_ready, 1)

            def exps(b, i):
                u = SLOTS * b + i
                act.wait_ge(st_mm, u + 1)
                if later(G * b + i // J - 1):
                    act.wait_ge(pv_mm, G * b + i // J - 1)
                act.activation(pt[i % PE_RING], bank[ST_BANK + i % 2][:], ACT.Exp, scale=SCALE)\
                 .then_inc(exp_done, 1)

            def attended(b, g):
                act.wait_ge(pv_mm, G * b + g + 1)
                if later(TB * b):
                    act.wait_ge(otr_mm, TB * b)
                act.activation(OT[:, g, :], bank[PV_BANK][:, (g % 2) * S:(g % 2 + 1) * S], ACT.Identity)\
                 .then_inc(ot_ready, 1)

            def concat_hi(b):
                act.wait_ge(cT_mm, b + 1)
                if later(b):
                    act.wait_ge(o_mm, b)
                act.activation(cch[:], bank[T_BANK][:, 0:S], ACT.Identity).then_inc(cch_ready, 1)

            def root2(part):
                act.wait_ge(std2_in, part + 1)
                act.activation(std2[:, part_tiles[part]], std2[:, part_tiles[part]], ACT.Sqrt).then_inc(std2_done, 1)

            def h2_parts(c):
                act.wait_ge(x2T_done, c + 1)
                if c >= 2:
                    act.wait_ge(h2l_ready, c - 1)
                for k in range(CW // S):
                    b = c * (CW // S) + k
                    src = bank[x2_bank(c)][:, k * S:(k + 1) * S]
                    act.activation(hf2[c % 2][:, k * S:(k + 1) * S], src, ACT.Identity, bias=mod[:, 3, b:b + 1],
                                 scale=mod1[:, 4, b:b + 1])
                    act.activation(H2h[:, c * CW + k * S:c * CW + (k + 1) * S], src, ACT.Identity,
                                 bias=mod[:, 3, b:b + 1], scale=mod1[:, 4, b:b + 1]).then_inc(h2_ready, 1)

            def gate_exp(part):
                act.wait_ge(lg_ready, part + 1)
                act.activation(sc[:, part_tiles[part]], lg[:, part_tiles[part]], ACT.Exp).then_inc(exp_gate, 1)

            def cwT_out(c):
                act.wait_ge(cwT_zero, 1)
                act.wait_ge(cwT_mm, c + 1)
                act.activation(cwT[0:NE, c * CW:(c + 1) * CW], bank[CWT_BANK[c]][0:NE, :], ACT.Identity)\
                 .then_inc(cwT_done, 1)

            act.wait_ge(cst_in, 3 * DMA)

            def body(b, par):
                last = isinstance(b, int) and b == NB - 1
                if last:
                    root2(0)
                for i in range(SLOTS):
                    if has(b, 0):
                        exps(b, i)
                    if last and i in ACT_H2:
                        h2_parts(ACT_H2.index(i))
                    if last and i == 12:
                        gate_exp(0)
                    if i == 1 and has(b, -1):
                        attended(b - 1, G - 1)
                    if i == H_AT and has(b, 2):
                        normed(b + 2, par)
                    if i in QK_AT and has(b, 2):
                        hi_part(b + 2, QK_AT.index(i))
                    if i == CHI_AT and has(b, -1):
                        concat_hi(b - 1)
                    if i in ATTEND_OUT_AT and has(b, 0):
                        attended(b, ATTEND_OUT_AT.index(i))
                    if i == V_OUT_AT and has(b, 1):
                        if isinstance(b, int) and b == -1:
                            act.wait_ge(idle_zero, 4)
                        values(b + 1, 1 - par)
                    if i == SLOTS - 2 and isinstance(b, int) and b == -2:
                        act.wait_ge(std_in, 2)
                        act.activation(std1[:, FIRST:NT], std1[:, FIRST:NT], ACT.Sqrt).then_inc(std_done, 1)
                    if i == 5 and isinstance(b, int) and b == -1:
                        act.wait_ge(ga_mm, 1)
                        for k in range(2):
                            act.activation(ga_b[:, 4 * k:4 * k + 4, :].rearrange("p a b -> p (a b)"),
                                           bank[ST_BANK + k][:], ACT.Identity).then_inc(ga_ready, 1)

            bodies(act, body)
            attended(NB - 1, G - 1)
            act.wait_ge(w13lo, NX)

            def chunk(c):
                for n in range(NX):
                    r = n % R
                    k = NX * c + n
                    act.wait_ge(g_mm, k + 1)
                    if later(k - R + 1):
                        act.wait_ge(pg_ready, k - R + 1)
                    act.activation(t1g[r], bank[2 * ((2 * n) % R)][:], ACT.Identity, bias=b13[:, n, 0:1])\
                     .then_inc(t1g_ready, 1)
                    if n > 0 or not isinstance(c, int):
                        sigmoid(c, n - 1) if n > 0 else sigmoid(c - 1, NX - 1)
                    if n == 2 and not isinstance(c, int):
                        scaled(c - 1)
                    act.wait_ge(l_mm, k + 1)
                    if later(k - R + 1):
                        act.wait_ge(pl_ready, k - R + 1)
                    act.activation(t1l[r], bank[2 * ((2 * n + 1) % R)][:], ACT.Identity, bias=b13[:, n, 1:2])\
                     .then_inc(t1l_ready, 1)
                    if isinstance(c, int):
                        if n == 0:
                            for early in range(EARLY):
                                cwT_out(early)
                        if n == 1:
                            concat_hi(NB - 1)
                        if n == 2:
                            root2(1)
                        if n == 4:
                            h2_parts(NC - 1)
                        if n == 5:
                            gate_exp(1)
                        if n == NX - 1:
                            cwT_out(NC - 1)
                            act.wait_ge(cwT_done, NC)
                            act.dma_start(cwd[:, EARLY * CW:NC * CW], cwT[0:NE, EARLY * CW:NC * CW])\
                             .then_inc(cw_late_out, DMA)

            def sigmoid(c, n):
                k = NX * c + n
                act.wait_ge(gm_ready, k + 1)
                if later(k - R + 1):
                    act.wait_ge(a_ready, k - R + 1)
                act.activation(sg[n % R], pg[n % R], ACT.Sigmoid, scale=ALPHA).then_inc(sg_ready, 1)

            def scaled(c):
                act.wait_ge(y_ready, c + 1)
                for k in range(CW // S):
                    b = c * (CW // S) + k
                    last = act.activation(zb[:, k * S:(k + 1) * S], bank[Y_BANK][:, k * S:(k + 1) * S], ACT.Identity,
                                        bias=gbias[:, bass.ds(b, 1)], scale=gb_t[:, bass.ds(b, 1)])
                last.then_inc(z_ready, 1)

            chunk(0)
            with act.Fori(1, NC) as c:
                chunk(c)
            sigmoid(NC - 1, NX - 1)
            scaled(NC - 1)

        @block.vector
        def _(dve):
            dve.wait_ge(silu_sig, 1)
            dve.tensor_tensor(siluT[:], cT[:], sigc[:], ALU.mult).then_inc(silu_done, 1)
            def stats1(tiles):
                for n in tiles:
                    if n % 4 == 0:
                        dve.wait_ge(x_in[n // 4], DMA)
                    last = dve.bn_stats(st1[:, n, :], xs[:, n, :])
                last.then_inc(st1_done, 1)

            def variances(group, tiles):
                for n in tiles:
                    last = dve.bn_aggr(mv1[:, n, :], st1[:, n, :])
                last.then_inc(mv1_done, 1)
                dve.wait_ge(mv1_done, group + 1)
                dve.tensor_scalar(std1[:, tiles[0]:NT if group else FIRST], mv1[:, tiles[0]:NT if group else FIRST, 1],
                                  EPS, None, ALU.add).then_inc(std_in, 1)

            stats1(range(FIRST))
            dve.wait_ge(st1_done, 1)
            variances(0, range(FIRST))
            dve.wait_ge(w4_in, DMA)
            dve.tensor_copy(w4h[:], w4[:]).then_inc(wsplit, 1)
            dve.memset(wrep[0][:].bitcast(fp32), 0.0)
            dve.memset(wrep[1][:].bitcast(fp32), 0.0).then_inc(wsplit, 1)
            dve.wait_ge(std_done, 1)
            dve.reciprocal(rstd1[:, 0:FIRST], std1[:, 0:FIRST]).then_inc(rstd_done, 1)
            dve.wait_ge(wsplit, 2)
            dve.tensor_tensor(w4l[:], w4[:], w4h[:].bitcast(fp32), ALU.subtract).then_inc(wsplit, 1)
            dve.wait_ge(mod_done, 1)
            dve.tensor_scalar(mod1[:], mod[:], 1.0, None, ALU.add).then_inc(mod_done, 1)
            dve.wait_ge(rstd_done, 1)

            def normalise(b):
                if later(b):
                    dve.wait_ge(xnT_done, b)
                for k in range(TB):
                    t = TB * b + k
                    last = dve.tensor_scalar(xn[:, k, :], xs[:, bass.ds(t, 1), :].rearrange("p a d -> p (a d)"),
                                           mv1[:, bass.ds(t, 1), 0], rstd1[:, bass.ds(t, 1)],
                                           ALU.subtract, ALU.mult)
                last.then_inc(xn_ready, 1)

            def h_lo(b, par):
                dve.wait_ge(h_ready, 2 * b + 2)
                dve.tensor_tensor(hl[par][:], hf[:], hh[par][:].bitcast(fp32), ALU.subtract).then_inc(hl_ready, 1)

            def stacked(b, n):
                dve.wait_ge(hi_ready, 4 * b + n + 1)
                if later(G * b):
                    dve.wait_ge(copied, G * b - (2 if n < 2 else 0))
                qk, half = n % 2, n // 2
                dve.scalar_tensor_tensor(out=stage[:, qk, 2 * half:2 * half + 2, :].rearrange("p a b -> p (a b)"),
                                       in0=hiS[n % 2][:].bitcast(fp32).rearrange("p a b -> p (a b)"),
                                       scalar=cols[:, qk:qk + 1], in1=a_bank(b, n)[:], op0=ALU.mult, op1=ALU.add)\
                 .then_inc(stage_ready, 1)

            def maximum(b, par, i):
                u = SLOTS * b + i
                dve.wait_ge(s_mm, u + 1)
                if i == 0:
                    if later(2 * (b - 1)):
                        dve.wait_ge(mT_done, 2 * (b - 1))
                dve.tensor_reduce(out=M[:, par, i % 2, 2 * (i // 2):2 * (i // 2) + 2],
                                in_=bank[S_BANK + i % 2][:].rearrange("p (a k) -> p a k", a=2),
                                axis=AX.X, op=ALU.max, negate=True).then_inc(max_done, 1)

            def maxima_parts(b, half):
                dve.wait_ge(mT_done, 2 * b + half + 1)
                if later(4 * DMA * b):
                    dve.wait_ge(mrow[half], 4 * DMA * b)
                dve.tensor_copy(mhl[:, half, 0, :], bank[T_BANK][0:8, 0:S]).then_inc(m_split, 1)
                dve.wait_ge(m_split, 4 * b + 2 * half + 1)
                dve.tensor_tensor(mhl[:, half, 1, :], bank[T_BANK][0:8, 0:S], mhl[:, half, 0, :].bitcast(fp32),
                                ALU.subtract).then_inc(m_split, 1)

            def divided(b, qt):
                dve.wait_ge(otr_mm, TB * b + qt + 1)
                if later(b):
                    dve.wait_ge(cT_mm, b)
                o = bank[o_bank(b, qt)][:].rearrange("p (h r) -> p h r", h=H)
                dve.reciprocal(rd[:, qt, :], o[:, :, HD]).then_inc(rd_ready, 1)
                dve.wait_ge(rd_ready, TB * b + qt + 1)
                dve.tensor_tensor(cc[:, qt, :].rearrange("p (h d) -> p h d", h=H), o[:, :, 0:HD],
                                rd[:, qt, :].unsqueeze(2).to_broadcast([P, H, HD]), ALU.mult).then_inc(cc_ready, 1)

            def concat_lo(b):
                dve.wait_ge(cch_ready, b + 1)
                dve.tensor_tensor(ccl[:], bank[T_BANK][:, 0:S], cch[:].bitcast(fp32), ALU.subtract)\
                 .then_inc(ccl_ready, 1)

            def residual(b):
                dve.wait_ge(o_mm, b + 1)
                dve.tensor_tensor(rt[:], out_psum(b).rearrange("p (t d) -> p t d", t=TB),
                                ga_b[:, bass.ds(b, 1), :].to_broadcast([P, TB, D]), ALU.mult)\
                 .then_inc(rt_ready, 1)
                dve.wait_ge(rt_ready, b + 1)
                xt = xs[:, bass.ds(TB * b, TB), :]
                dve.tensor_tensor(xt, rt[:], xt, ALU.add).then_inc(x2_ready, 1)

            def stats2(b):
                dve.wait_ge(x2_ready, b + 1)
                for k in range(TB):
                    t = TB * b + k
                    last = dve.bn_stats(st2[:, bass.ds(t, 1), :].rearrange("p a k -> p (a k)"),
                                      xs[:, bass.ds(t, 1), :].rearrange("p a d -> p (a d)"))
                last.then_inc(st2_done, 1)

            def guards():
                g = mod[:, 2:6:3, :]
                dve.tensor_scalar(gneg[:], g, -1.0, None, ALU.mult).then_inc(g_chain, 1)
                dve.tensor_scalar(gsgn[:], g, 0.0, 2.0, ALU.is_ge, ALU.mult).then_inc(g_chain, 1)
                dve.wait_ge(g_chain, 2)
                dve.tensor_tensor(gabs[:], gneg[:], g, ALU.max).then_inc(g_chain, 1)
                dve.wait_ge(g_chain, 3)
                dve.tensor_scalar(gneg[:], gabs[:], 0.25, None, ALU.max).then_inc(g_chain, 1)
                dve.wait_ge(g_chain, 4)
                dve.scalar_tensor_tensor(out=gt[:], in0=gsgn[:], scalar=-1.0, in1=gneg[:], op0=ALU.add,
                                         op1=ALU.mult).then_inc(g_chain, 1)
                dve.wait_ge(g_chain, 5)
                dve.tensor_copy(gaB[:], gt[:, 0, :].unsqueeze(2).to_broadcast([P, NB, P])).then_inc(gaB_ready, 1)
                dve.wait_ge(small_in, 5 * DMA)
                dve.tensor_scalar(gbias[:], gb_t, sb2[:, 0:1], None, ALU.mult).then_inc(gb_ready, 1)
                dve.tensor_copy(gwh[:], gwT[:]).then_inc(gwsplit, 1)
                dve.wait_ge(gwsplit, 1)
                dve.tensor_tensor(gwl[:], gwT[:], gwh[:].bitcast(fp32), ALU.subtract).then_inc(gwsplit, 1)

            def replicated():
                dve.wait_ge(wsplit, 3)
                for n, w in enumerate((w4h, w4l)):
                    for c in range(3):
                        last = dve.tensor_copy(wrep[n][:, :, :, c, :],
                                               w[:, 0:2, :].bitcast(fp32).rearrange("p a (h d) -> p a h d", h=H))
                last.then_inc(wrep_done, 1)

            def variances2(part):
                rows = (EARLY * CW, NC * CW)[part] // S
                dve.wait_ge(st2_done, rows)
                for t in range(NT)[part_tiles[part]]:
                    last = dve.bn_aggr(mv2[:, t, :], st2[:, t, :])
                last.then_inc(mv2_done, 1)
                dve.wait_ge(mv2_done, part + 1)
                dve.tensor_scalar(std2[:, part_tiles[part]], mv2[:, part_tiles[part], 1], EPS, None, ALU.add)\
                 .then_inc(std2_in, 1)

            def inverse2(part):
                dve.wait_ge(std2_done, part + 1)
                dve.reciprocal(rstd2[:, part_tiles[part]], std2[:, part_tiles[part]]).then_inc(rstd2_done, 1)
                dve.wait_ge(rstd2_done, part + 1)

            def normalise2(c):
                if c >= 2:
                    dve.wait_ge(x2T_done, c - 1)
                for k in range(CT):
                    t = c * CT + k
                    last = dve.tensor_scalar(xn2[c % 2][:, k * P:(k + 1) * P], xs[:, t, :], mv2[:, t, 0:1],
                                           rstd2[:, t:t + 1], ALU.subtract, ALU.mult)
                last.then_inc(xn2_ready, 1)

            def h2_lo(c):
                dve.wait_ge(h2_ready, 2 * c + 2)
                dve.tensor_tensor(H2l[:, c * CW:(c + 1) * CW], hf2[c % 2],
                                H2h[:, c * CW:(c + 1) * CW].bitcast(fp32), ALU.subtract).then_inc(h2l_ready, 1)

            step = [0]

            def link(ins):
                step[0] += 1
                ins.then_inc(route, 1)
                dve.wait_ge(route, step[0])

            def per_token(v, T):
                return v[:, T].unsqueeze(2).to_broadcast([P, T.stop - T.start, NE])

            def per_expert(v, T):
                return v[:].unsqueeze(1).to_broadcast([P, T.stop - T.start, NE])

            def logits_less_max(part):
                T = part_tiles[part]
                dve.wait_ge(gate_mm, part + 1)
                logits = bank[GATE_BANK[part]][:, T.start * NE:T.stop * NE].rearrange("p (t n) -> p t n", n=NE)
                link(dve.tensor_reduce(out=r1[0][:, T], in_=logits, axis=AX.X, op=ALU.max))
                dve.tensor_tensor(lg[:, T], logits, per_token(r1[0], T), ALU.subtract).then_inc(lg_ready, 1)

            def expert_scores(part):
                T = part_tiles[part]
                dve.wait_ge(exp_gate, part + 1)
                link(dve.tensor_reduce(out=r1[1][:, T], in_=sc[:, T], axis=AX.X, op=ALU.add))
                link(dve.reciprocal(r1[2][:, T], r1[1][:, T]))
                link(dve.tensor_tensor(lg[:, T], sc[:, T], per_token(r1[2], T), ALU.mult))
                link(dve.tensor_tensor(bi[:, T], lg[:, T], per_expert(gbb, T), ALU.add))

            def top(part, n):
                T = part_tiles[part]
                value, index = r1[3 + 2 * n], r1[4 + 2 * n]
                if n == 1:
                    link(dve.scalar_tensor_tensor(out=bi[:, T], in0=oh[0][:, T], scalar=-3.0e38, in1=bi[:, T],
                                                op0=ALU.mult, op1=ALU.add))
                link(dve.tensor_reduce(out=value[:, T], in_=bi[:, T], axis=AX.X, op=ALU.max))
                link(dve.tensor_tensor(eq[:, T], bi[:, T], per_token(value, T), ALU.is_ge))
                link(dve.tensor_tensor(cw[:, T], eq[:, T], per_expert(rev, T), ALU.mult))
                link(dve.tensor_reduce(out=index[:, T], in_=cw[:, T], axis=AX.X, op=ALU.max))
                link(dve.tensor_tensor(oh[n][:, T], cw[:, T], per_token(index, T), ALU.is_equal))

            def expert_weights(part):
                T = part_tiles[part]
                link(dve.tensor_tensor(eq[:, T], oh[0][:, T], oh[1][:, T], ALU.add))
                dve.tensor_tensor(cw[:, T], eq[:, T], lg[:, T], ALU.mult).then_inc(cw_done, 1)

            dve.wait_ge(cst_in, 3 * DMA)

            def body(b, par):
                last = isinstance(b, int) and b == NB - 1
                for i in range(SLOTS):
                    if i == 0 and has(b, 2):
                        normalise(b + 2)
                    if has(b, 1):
                        maximum(b + 1, 1 - par, i)
                    if i == 1 and last:
                        maxima_parts(b, 1)
                        inverse2(0)
                    if isinstance(b, int) and b == -2:
                        if i == 0:
                            replicated()
                        if i == 12:
                            stats1(range(FIRST, NT))
                            dve.wait_ge(st1_done, 2)
                            variances(1, range(FIRST, NT))
                    if isinstance(b, int) and b == -1:
                        if i == 1:
                            dve.wait_ge(std_done, 2)
                            dve.reciprocal(rstd1[:, FIRST:NT], std1[:, FIRST:NT]).then_inc(rstd_done, 1)
                            dve.wait_ge(rstd_done, 2)
                            guards()
                    if i == PARTS1_AT and has(b, 0) and not last:
                        maxima_parts(b, 1)
                    if i == HL_AT and has(b, 2):
                        h_lo(b + 2, par)
                    if i in DIV_AT and has(b, -1):
                        divided(b - 1, DIV_AT.index(i))
                    if i in STACK_AT and has(b, 2):
                        stacked(b + 2, STACK_AT.index(i))
                    if i == CLO_AT and has(b, -1):
                        concat_lo(b - 1)
                    if i == PARTS0_AT and has(b, 1):
                        maxima_parts(b + 1, 0)
                    if i == RES_AT and has(b, -1):
                        residual(b - 1)
                    if i == ST2_AT and has(b, -1):
                        stats2(b - 1)
                    if isinstance(b, int) and b == NB - 2 and i == ST2_AT:
                        variances2(0)
                    if last and i in DVE_XN2:
                        normalise2(DVE_XN2.index(i))
                    if last and i in DVE_H2L:
                        h2_lo(DVE_H2L.index(i))
                    if last and i == 12:
                        logits_less_max(0)
                    if last and i == 15:
                        expert_scores(0)
                        top(0, 0)
                        top(0, 1)
                        expert_weights(0)

            bodies(dve, body)

            def chunk(c):
                for n in range(NX):
                    r = n % R
                    k = NX * c + n
                    dve.wait_ge(t1g_ready, k + 1)
                    if later(k - R + 1):
                        dve.wait_ge(sg_ready, k - R + 1)
                    if later(x_before(c, n)):
                        dve.wait_ge(x_ready, x_before(c, n))
                    dve.scalar_tensor_tensor(out=pg[r], in0=bank[2 * ((2 * n) % R) + 1][:], scalar=b13[:, n, 2:3],
                                           in1=t1g[r], op0=ALU.add, op1=ALU.mult).then_inc(pg_ready, 1)
                    dve.wait_ge(pg_ready, k + 1)
                    dve.tensor_scalar(pg[r], pg[r], LIMIT, None, ALU.min).then_inc(gm_ready, 1)
                    if n > 0 or not isinstance(c, int):
                        weighted(c, n - 1) if n > 0 else weighted(c - 1, NX - 1)
                    dve.wait_ge(t1l_ready, k + 1)
                    dve.scalar_tensor_tensor(out=pl[r], in0=bank[2 * ((2 * n + 1) % R) + 1][:], scalar=b13[:, n, 3:4],
                                           in1=t1l[r], op0=ALU.add, op1=ALU.mult).then_inc(pl_ready, 1)
                    dve.wait_ge(pl_ready, k + 1)
                    dve.tensor_scalar(pl[r], pl[r], -LIMIT, LIMIT, ALU.max, ALU.min).then_inc(lc_ready, 1)
                    if n == 4 and not isinstance(c, int):
                        finish(c - 1)
                    if isinstance(c, int):
                        if n == 0:
                            divided(NB - 1, 0)
                            divided(NB - 1, 1)
                        if n == 1:
                            concat_lo(NB - 1)
                        if n == 2:
                            residual(NB - 1)
                            stats2(NB - 1)
                            variances2(1)
                        if n == 3:
                            inverse2(1)
                            normalise2(NC - 1)
                        if n == 4:
                            h2_lo(NC - 1)
                        if n == 5:
                            logits_less_max(1)
                        if n == 6:
                            expert_scores(1)
                            top(1, 0)
                        if n == 7:
                            top(1, 1)
                            expert_weights(1)

            def weighted(c, n):
                r = n % R
                k = NX * c + n
                dve.wait_ge(lc_ready, k + 1)
                if n > 0:
                    dve.wait_ge(x_ready, NE * c + n)
                else:
                    if later(k - R + 1):
                        dve.wait_ge(a_ready, k - R + 1)
                dve.scalar_tensor_tensor(out=X[r], in0=pl[r], scalar=1.0, in1=X[r] if n > 0 else pg[r],
                                       op0=ALU.add, op1=ALU.mult).then_inc(yx_ready, 1)

            def finish(c):
                dve.wait_ge(zT_done, c + 1)
                dve.wait_ge(dram_out, DMA * (c + 1))
                dve.tensor_tensor(yo, bank[Z_BANK][:].rearrange("p (t d) -> p t d", t=CT),
                                xs[:, bass.ds(c * CT, CT), :], ALU.add).then_inc(yo_ready, 1)

            dve.wait_ge(w13lo, NX)
            dve.wait_ge(pv_mm, G * NB)
            chunk(0)
            with dve.Fori(1, NC) as c:
                chunk(c)
            weighted(NC - 1, NX - 1)
            finish(NC - 1)

        @block.tensor
        def _(pe):
            def product(out, hi, lo, rhi, rlo):
                pe.matmul(out, hi, rhi, start=True, stop=False)
                pe.matmul(out, lo, rhi, start=False, stop=False)
                return pe.matmul(out, hi, rlo, start=False, stop=True)

            pe.wait_ge(silu_done, 1)
            pe.wait_ge(c_in, 2 * DMA)
            for k in range(6):
                last = pe.matmul(bank[0][:, k * NB:(k + 1) * NB], wmod[:, k, :], siluT[:], start=True, stop=True)
            last.then_inc(mod_mm, 1)

            def normedT(b):
                pe.wait_ge(xn_ready, b + 1)
                if later(b - 1):
                    pe.wait_ge(v_ready, b - 1)
                if later(b - 3):
                    pe.wait_ge(rt_ready, b - 3)
                if isinstance(b, int) and b == 1:
                    pe.wait_ge(stage_ready, 4)
                for k in range(TB):
                    last = pe.transpose(half_bank[:, k * P:(k + 1) * P], xn[:, k, :], ident[:])
                last.then_inc(xnT_done, 1)

            def qk_step(b, par, n):
                pe.wait_ge(hl_ready, b + 1)
                if later(4 * b + n) and not (isinstance(b, int) and b == 0):
                    pe.wait_ge(stage_ready, 4 * b + n)
                qk, half = n % 2, n // 2
                for k in range(2):
                    g = 2 * half + k
                    wh = wrep[0][:, qk, J * g:J * g + J].rearrange("p h c d -> p (h c d)")
                    wl = wrep[1][:, qk, J * g:J * g + J].rearrange("p h c d -> p (h c d)")
                    last = product(a_bank(b, n)[:, k * S:(k + 1) * S], wh, wl, hh[par][:], hl[par][:])
                last.then_inc(qk_mm, 1)

            def values(b, par):
                if later(TB * (b - 1)):
                    pe.wait_ge(cc_ready, TB * (b - 1))
                elif b + 1 < NB:
                    pe.wait_ge(h_ready, 2 * (b + 2))
                for k in range(TB):
                    tk = slice(k * P, (k + 1) * P)
                    last = product(half_bank[:, k * D:(k + 1) * D], hh[par][:, tk], hl[par][:, tk],
                                   w4h[:, 2, :], w4l[:, 2, :])
                last.then_inc(v_mm, 1)

            def scores_q(b, par, i):
                u = SLOTS * b + i
                pair, qt = i // 2, i % 2
                g = pair // 2
                if i % 4 == 0:
                    pe.wait_ge(copied, G * b + g + 1)
                if later(u - 1):
                    pe.wait_ge(max_done, u - 1)
                pe.matmul(bank[S_BANK + i % 2][:], Qst[par][:, g, qt * P:(qt + 1) * P],
                         Kx[:, par, 2 * pair:2 * pair + 2, :].rearrange("p a b -> p (a b)"),
                         start=True, stop=True).then_inc(s_mm, 1)

            def scores_k(b, par, h):
                u = SLOTS * b + h
                if h % (H // 2) == 0:
                    pe.wait_ge(mrow[h // (H // 2)], 4 * DMA * (b + 1))
                if later(u - 1):
                    pe.wait_ge(exp_done, u - 1)
                for k in range(TB):
                    last = pe.matmul(bank[ST_BANK + h % 2][:, k * S:(k + 1) * S], Kx[:, par, h, k * P:(k + 1) * P],
                                    Qst[par][:, h // J, :], start=True, stop=True)
                last.then_inc(st_mm, 1)

            def attend(b, par, g):
                pe.wait_ge(exp_done, SLOTS * b + J * g + J)
                pe.wait_ge(v_ready, b + 1)
                if later(G * b + g - 1):
                    pe.wait_ge(ot_ready, G * b + g - 1)
                for k in range(TB):
                    for j in range(J):
                        h = J * g + j
                        last = pe.matmul(bank[PV_BANK][32 * j:32 * j + 32, (g % 2) * S:(g % 2 + 1) * S],
                                        V[par][:, k, h, :], pt[h % PE_RING][:, k * S:(k + 1) * S],
                                        start=k == 0, stop=k == TB - 1, skip_group_check=True)
                last.then_inc(pv_mm, 1)

            def maximaT(b, par, half):
                pe.wait_ge(max_done, SLOTS * b + 8 * half + 8)
                if half == 1:
                    pe.wait_ge(m_split, 4 * b + 2)
                    if later(b - 1):
                        pe.wait_ge(ccl_ready, b - 1)
                elif not (isinstance(b, int) and b == 0):
                    pe.wait_ge(m_split, 4 * b)
                for k in range(TB):
                    last = pe.transpose(bank[T_BANK][0:8, k * P:(k + 1) * P],
                                       M[:, par, k, 8 * half:8 * half + 8], ident[:])
                last.then_inc(mT_done, 1)

            def attendedT(b, qt):
                pe.wait_ge(ot_ready, G * b + G)
                if later(b):
                    pe.wait_ge(rt_ready, b)
                if not isinstance(b, int) or b + 3 < NB:
                    pe.wait_ge(h_ready, 2 * (b + 4))
                if isinstance(b, int) and b == NB - 1:
                    pe.wait_ge(cwT_done, EARLY)
                elif later(TB * b + qt):
                    pe.wait_ge(cc_ready, TB * b + qt)
                if isinstance(b, int) and b == 0:
                    pe.wait_ge(ga_ready, 2)
                for g in range(G):
                    last = pe.transpose(bank[o_bank(b, qt)][:, g * P:(g + 1) * P], OT[:, g, qt * P:(qt + 1) * P], ident[:])
                last.then_inc(otr_mm, 1)

            def concatT(b):
                pe.wait_ge(cc_ready, TB * b + TB)
                if later(b):
                    pe.wait_ge(ccl_ready, b)
                if isinstance(b, int) and b == NB - 2:
                    pe.wait_ge(m_split, 4 * NB)
                elif not (isinstance(b, int) and b == NB - 1):
                    pe.wait_ge(m_split, 4 * (b + 2) + 2)
                for k in range(TB):
                    last = pe.transpose(bank[T_BANK][:, k * P:(k + 1) * P], cc[:, k, :], ident[:])
                last.then_inc(cT_mm, 1)

            def output(b):
                pe.wait_ge(ccl_ready, b + 1)
                if not isinstance(b, int) or b + 2 < NB:
                    pe.wait_ge(v_ready, b + 3)
                for k in range(TB):
                    tk = slice(k * P, (k + 1) * P)
                    last = product(out_psum(b)[:, k * D:(k + 1) * D], cch[:, tk], ccl[:, tk],
                                   w4h[:, 3, :], w4l[:, 3, :])
                last.then_inc(o_mm, 1)

            def normed2T(c):
                pe.wait_ge(xn2_ready, c + 1)
                if c == 0:
                    pe.wait_ge(max_done, SLOTS * NB)
                if c >= 2:
                    pe.wait_ge(h2_ready, 2 * (c - 1))
                for k in range(CT):
                    last = pe.transpose(bank[x2_bank(c)][:, k * P:(k + 1) * P], xn2[c % 2][:, k * P:(k + 1) * P],
                                        ident[:])
                last.then_inc(x2T_done, 1)

            def gate(c):
                if c == 0:
                    pe.wait_ge(stage_ready, 4 * NB)
                    pe.wait_ge(gwsplit, 2)
                pe.wait_ge(h2l_ready, c + 1)
                for k in range(CT):
                    t = c * CT + k
                    tk = slice(t * P, (t + 1) * P)
                    last = product(bank[GATE_BANK[c // EARLY]][:, t * NE:(t + 1) * NE], H2h[:, tk], H2l[:, tk],
                                   gwh[:], gwl[:])
                if c >= EARLY - 1:
                    last.then_inc(gate_mm, 1)

            def cwT_chunk(c):
                if c == 1:
                    pe.wait_ge(rt_ready, NB - 1)
                for k in range(CT):
                    last = pe.transpose(bank[CWT_BANK[c]][0:NE, k * P:(k + 1) * P], cw[:, c * CT + k, :], ident[:])
                last.then_inc(cwT_mm, 1)

            pe.wait_ge(cst_in, 3 * DMA)

            def body(b, par):
                last_body = isinstance(b, int) and b == NB - 1
                for i in range(SLOTS):
                    if has(b, 1):
                        scores_q(b + 1, 1 - par, i)
                    if has(b, 0):
                        scores_k(b, par, i)
                    if i == 1 and has(b, -1):
                        attend(b - 1, 1 - par, G - 1)
                    if i == MAXT1_AT and has(b, 0):
                        maximaT(b, par, 1)
                    if i == 4 and isinstance(b, int) and b == -2:
                        pe.wait_ge(wrep_done, 1)
                    if i == 4 and isinstance(b, int) and b == -1:
                        pe.wait_ge(gaB_ready, 1)
                        for k in range(NB):
                            last = pe.matmul(bank[ST_BANK + k // 4][:, (k % 4) * D:(k % 4 + 1) * D], gaB[:, k, :],
                                             ident[:], start=True, stop=True)
                        last.then_inc(ga_mm, 1)
                    if i == XNT_AT and has(b, 2):
                        normedT(b + 2)
                    if i in OT_AT and has(b, -1):
                        attendedT(b - 1, OT_AT.index(i))
                    if i in QK_AT and has(b, 2):
                        qk_step(b + 2, par, QK_AT.index(i))
                    if i in ATTEND_AT and has(b, 0):
                        attend(b, par, ATTEND_AT.index(i))
                    if i == CT_AT and has(b, -1):
                        concatT(b - 1)
                    if i == OUT_AT and has(b, -1):
                        output(b - 1)
                    if i == MAXT0_AT and has(b, 1):
                        maximaT(b + 1, 1 - par, 0)
                    if i == V_AT and has(b, 1):
                        values(b + 1, 1 - par)
                    if last_body and i in PE_X2T:
                        normed2T(PE_X2T.index(i))
                    if last_body and i in PE_GATE:
                        gate(PE_GATE.index(i))

            bodies(pe, body)
            attend(NB - 1, (NB - 1) % 2, G - 1)

            def first_layer(c, n):
                rhi, rlo = H2h[:, bass.ds(c * CW, CW)], H2l[:, bass.ds(c * CW, CW)]
                for part, done in ((0, g_mm), (1, l_mm)):
                    u = 2 * n + part
                    prev = u - R
                    k = NX * c + prev // 2
                    if isinstance(c, int) and u == 1:
                        pe.wait_ge(exp_done, SLOTS * NB)
                    if isinstance(c, int) and u == 2:
                        pe.wait_ge(ot_ready, G * NB)
                        pe.wait_ge(cwT_done, 1)
                    if later(k + 1) and prev % 2:
                        pe.wait_ge(pl_ready, k + 1)
                    elif later(k + 1):
                        pe.wait_ge(pg_ready, k + 1)
                    for m in range(2):
                        w = slice((2 * m + part) * P, (2 * m + part + 1) * P)
                        last = product(bank[2 * (u % R) + m][:], w13h[:, n, w], w13l[:, n, w], rhi, rlo)
                    last.then_inc(done, 1)

            def second_layer(c, n):
                pe.wait_ge(a_ready, NX * c + n + 1)
                if n == 0:
                    if later(c):
                        pe.wait_ge(z_ready, c)
                pe.matmul(bank[Y_BANK][:], w2[:, n, :], av[n % R], start=n == 0, stop=False).then_inc(w2_mm, 1)
                if n == NX - 1:
                    pe.matmul(bank[Y_BANK][:], b2[:], cwT[:, bass.ds(c * CW, CW)], start=False, stop=True)\
                     .then_inc(y_ready, 1)

            def backT(c):
                pe.wait_ge(z_ready, c + 1)
                for k in range(CT):
                    last = pe.transpose(bank[Z_BANK][:, k * P:(k + 1) * P], zb[:, k * P:(k + 1) * P], ident[:])
                last.then_inc(zT_done, 1)

            LAG = 2

            def beside_first_chunk(n):
                if n == 0:
                    pe.wait_ge(cw_done, 1)
                    for c in range(EARLY):
                        cwT_chunk(c)
                    attendedT(NB - 1, 0)
                    attendedT(NB - 1, 1)
                if n == 1:
                    concatT(NB - 1)
                if n == 2:
                    output(NB - 1)
                if n == 4:
                    normed2T(NC - 1)
                if n == 5:
                    gate(NC - 1)
                if n == NX - 1:
                    pe.wait_ge(cw_done, 2)
                    cwT_chunk(NC - 1)

            def chunk(c):
                for n in range(NX):
                    first_layer(c, n)
                    if isinstance(c, int):
                        beside_first_chunk(n)
                    if n >= LAG:
                        second_layer(c, n - LAG)
                    elif not isinstance(c, int):
                        second_layer(c - 1, NX + n - LAG)
                    if n == 3 and not isinstance(c, int):
                        backT(c - 1)

            pe.wait_ge(w13lo, NX)
            pe.wait_ge(w2_in, DMA)
            pe.wait_ge(small_in, 5 * DMA)
            chunk(0)
            with pe.Fori(1, NC) as c:
                chunk(c)
            for n in range(NX - LAG, NX):
                second_layer(NC - 1, n)
            backT(NC - 1)


def kernel(**inputs):
    import numpy as np
    import concourse.bacc as _bacc
    from concourse import mybir as _mybir
    from concourse.bass_utils import run_bass_kernel_spmd as _run

    a = {k: np.asarray(v) for k, v in inputs.items()}
    x = a["L0_attn_x"]
    B, S, D = x.shape
    P = 128
    NT = B * S // P
    x_l = x.reshape(NT, P, D).transpose(1, 0, 2)
    w4 = np.stack([a["L0_attn_w_" + n].T for n in "qkvo"], axis=1)
    E, F2, _ = a["L0_ffn_w1"].shape
    w1 = np.concatenate([a["L0_ffn_sw1"][None], a["L0_ffn_w1"]])
    w3 = np.concatenate([a["L0_ffn_sw3"][None], a["L0_ffn_w3"]])
    w13 = np.concatenate([w1[:, 0::2], w1[:, 1::2], w3[:, 0::2], w3[:, 1::2]], axis=1).transpose(2, 0, 1)
    b1 = np.concatenate([a["L0_ffn_sb1"][None], a["L0_ffn_b1"]])
    b3 = np.concatenate([a["L0_ffn_sb3"][None], a["L0_ffn_b3"]])
    b13 = np.stack([b1[:, 0::2], b1[:, 1::2], b3[:, 0::2], b3[:, 1::2]], axis=1).transpose(2, 0, 1)
    w2 = np.concatenate([a["L0_ffn_sw2"][None], a["L0_ffn_w2"]]).transpose(2, 0, 1)
    row = np.arange(P) % 32
    c = row // 8
    one = row // 2 == 12
    cols = np.stack([np.where(c == 1, -1.0, 0.0), np.where(c == 2, -1.0, np.where(one, 1.0, 0.0)),
                     np.where(one, 1.0, 0.0)] + [np.where(np.arange(P) // 32 == j, 1.0, 0.0) for j in range(4)],
                    axis=1).astype(np.float32)
    ins = {
        "x": x_l, "w4": w4, "cT": a["L0_c"].T, "wmod": a["L0_wmod"].reshape(D, 6, D), "w13": w13, "w2": w2,
        "b13": b13, "b2": a["L0_ffn_b2"], "sb2": a["L0_ffn_sb2"].reshape(D, 1), "gw": a["L0_ffn_gate_w"].T,
        "gb": a["L0_ffn_gate_b"], "ident": np.eye(P, dtype=np.float32), "cols": cols,
        "rev": np.ascontiguousarray(np.broadcast_to(np.arange(E, 0, -1, dtype=np.float32), (P, E))),
    }
    nc = _bacc.Bacc("TRN2", target_bir_lowering=False, num_devices=1)
    arrays, args = {}, []
    for name, v in ins.items():
        v = np.ascontiguousarray(v)
        arrays[f"in_{name}"] = v
        args.append(nc.dram_tensor(f"in_{name}", v.shape, _mybir.dt.from_np(v.dtype), kind="ExternalInput").ap())
    args.append(nc.dram_tensor("out_y", (P, NT, D), _mybir.dt.float32, kind="ExternalOutput").ap())
    block_kernel(nc, *args)
    r = _run(nc, [arrays], core_ids=[0])
    y = r.results[0]["out_y"]
    return y.transpose(1, 0, 2).reshape(B, S, D)
```

```python
from contextlib import ExitStack

import concourse.bass as bass
from concourse import mybir


def block_kernel(nc, x_d, w4_d, cT_d, wmod_d, w13_d, w2_d, b13_d, b2_d, sb2_d, gw_d, gb_d, ident_d, cols_d, rev_d, y_d):
    fp32, f32r = mybir.dt.float32, mybir.dt.float32r
    ALU, ACT, AX = mybir.AluOpType, mybir.ActivationFunctionType, mybir.AxisListType
    P = 128
    D = x_d.shape[2]
    NT = x_d.shape[1]
    NB = cT_d.shape[1]
    TB = NT // NB
    S = TB * P
    HD = 8
    H = D // HD
    G = 4
    J = H // G
    SCALE = float(HD) ** -0.5
    EPS = 1e-5
    NE = gw_d.shape[1]
    NX = NE + 1
    CT = 4
    CW = CT * P
    NC = NT // CT
    ALPHA, LIMIT = 1.702, 7.0
    SLOTS = H
    QK_AT, QKB_AT = (5, 8, 11, 14), (5, 8, 11, 14)
    HI_AT, STACK_AT = (5, 8, 11, 14), (6, 9, 12, 15)
    ATTENDB_AT, FOURTHB_AT = (5, 9, 13), 0
    XNT_AT, H_AT, HL_AT = 2, 3, 3
    V_AT, V_OUT_AT = 10, 11
    ATTEND_AT, ATTEND_OUT_AT = (5, 9, 13), (5, 10, 14)
    FOURTH_AT, FOURTH_OUT_AT = 0, 1
    MAXT1_AT, PARTS1_AT = 0, 1
    MAXT0_AT, PARTS0_AT = 9, 11
    OT_AT, DIV_AT = (5, 7), (4, 8)
    CT_AT, CHI_AT, CLO_AT = 13, 13, 13
    QK1_AT, STACK1_AT = (2, 4, 6, 8), (2, 4, 6, 8)
    XNT1_AT, H1_AT, HL1_AT = 0, 0, 0
    STD_AT, RSTD_AT = 2, 4
    GUARD_AT, GAB_AT, GA_AT, GA_OUT_AT = 2, 9, 12, 14
    MHI0_AT, MHI1_AT = 9, 0
    X2T_AT, GATE_AT = (4, 6, 7), (8, 9, 11)
    ROOT_AT, H2_AT, GEXP_AT = 1, (4, 6, 8), 12
    VAR_AT, XN2_AT, H2L_AT = 1, (2, 3, 4), (6, 7, 8)
    LOG_AT, TOP_AT = 12, 13
    OT_BY, DIV_BY, CT_BY, CHI_BY, CLO_BY = 2, 1, 3, 2, 2
    OUT_BY, RES_BY, VAR_BY, ROOT_BY, XN2_BY = 5, 4, 4, 7, 7
    X2T_BY, H2_BY, H2L_BY, GATE_BY, LOG_BY = 10, 10, 10, 12, 12
    GEXP_BY, SCORE_BY, TOP_BY, CWT_BY, CWT_OUT_BY = 13, 13, 14, 17, 17
    EARLY_CWT_BY, EARLY_CWT_OUT_BY = 1, 1
    OUT_AT, RES_AT, ST2_AT = 15, 15, 1
    DMA = 16

    cwd = nc.dram_tensor("cw_scratch", (NE, NT * P), fp32, kind="Internal").ap()

    ctx = ExitStack()
    with ctx:
        def sb(name, shape, dt=fp32):
            return ctx.enter_context(nc.sbuf_tensor(name, shape, dt))

        def sem(name):
            return ctx.enter_context(nc.semaphore(name))

        xs = sb("xs", [P, NT, D])
        w4 = sb("w4", [P, 4, P])
        w4h = sb("w4h", [P, 4, P], f32r)
        w4l = sb("w4l", [P, 4, P], f32r)
        wrep = [sb(f"wrep{n}", [P, 2, H, 4, HD], f32r) for n in range(2)]
        cT = sb("cT", [P, NB])
        sigc = sb("sigc", [P, NB])
        siluT = sb("siluT", [P, NB])
        gaB = sb("gaB", [P, NB, P])
        mod = sb("mod", [P, 6, NB])
        mod1 = sb("mod1", [P, 6, NB])
        gneg = sb("gneg", [P, 2, NB])
        gabs = sb("gabs", [P, 2, NB])
        gsgn = sb("gsgn", [P, 2, NB])
        gt = sb("gt", [P, 2, NB])
        gb_t = gt[:, 1, :]
        gbias = sb("gbias", [P, NB])
        ga_b = sb("ga_b", [P, NB, D])
        st1 = sb("st1", [P, NT, 6])
        mv1 = sb("mv1", [P, NT, 2])
        std1 = sb("std1", [P, NT])
        rstd1 = sb("rstd1", [P, NT])
        shift1 = sb("shift1", [P, NT])
        ident = sb("ident", [P, P])
        cols = sb("cols", [P, 3 + J])
        rev = sb("rev", [P, NE])
        zcol = sb("zcol", [P, 1])
        xn = sb("xn", [P, TB, D])
        hf = sb("hf", [P, S])
        hh = [sb(f"hh{n}", [P, S], f32r) for n in range(2)]
        hl = [sb(f"hl{n}", [P, S], f32r) for n in range(2)]
        hiS = [sb(f"hiS{n}", [P, 2, S], f32r) for n in range(2)]
        stage = sb("stage", [P, 2, G, S], f32r)
        Qst = [sb(f"Qst{n}", [P, G, S], f32r) for n in range(2)]
        Kx = sb("Kx", [P, 2, H, S], f32r)
        Vb = sb("Vb", [P, 2, TB, H, 32])
        V = [Vb[:, n] for n in range(2)]
        M = sb("M", [P, 2, TB, H])
        mhl = sb("mhl", [8, 2, 2, S], f32r)
        OT = sb("OT", [P, 2, G, S])
        rd = sb("rd", [P, TB, H])
        cc = sb("cc", [P, TB, D])
        cch = sb("cch", [P, S], f32r)
        ccl = sb("ccl", [P, S], f32r)
        rt = sb("rt", [P, TB, D])
        st2 = sb("st2", [P, NT, 6])
        mv2 = sb("mv2", [P, NT, 2])
        std2 = sb("std2", [P, NT])
        rstd2 = sb("rstd2", [P, NT])
        w13h = sb("w13h", [P, NX, 4 * P], f32r)
        w13l = sb("w13l", [P, NX, 4 * P], f32r)
        w2 = sb("w2", [P, NX, P])
        b13 = sb("b13", [P, NX, 4])
        b2 = sb("b2", [P, D])
        sb2 = sb("sb2", [P, 1])
        gwT = sb("gwT", [P, NE])
        gwh = sb("gwh", [P, NE], f32r)
        gwl = sb("gwl", [P, NE], f32r)
        gbb = sb("gbb", [P, NE])
        NF = 21
        F = sb("F", [P, NF, CW])
        w13 = F[:, 0:NX, :]
        PE_RING = 8
        pt = [F[:, NX + n, :] for n in range(PE_RING)]
        R = 3
        t1g, t1l, pg, pl, X, sg, av = [[F[:, R * k + n, :] for n in range(R)] for k in range(7)]
        cwB = sb("cwB", [P, R, CW])
        H2h = Kx[:, 0, 0:H // 2, :].rearrange("p a b -> p (a b)")
        H2l = Kx[:, 0, H // 2:H, :].rearrange("p a b -> p (a b)")
        wmod = F[:, NX + PE_RING + 2:NX + PE_RING + 4, :].rearrange("p a b -> p (a b)")[:, 0:6 * D]\
            .rearrange("p (a b) -> p a b", a=6)
        cwT = stage[:].bitcast(fp32).rearrange("p a g s -> p (a g s)")
        xn2 = [hiS[n][:].bitcast(fp32).rearrange("p a b -> p (a b)") for n in range(2)]
        hf2 = [gaB[:, 0:4, :].rearrange("p a b -> p (a b)"), gaB[:, 4:8, :].rearrange("p a b -> p (a b)")]
        zb = ga_b[:, 0:4, :].rearrange("p a b -> p (a b)")
        yo = ga_b[:, 4:8, :]
        lg = sb("lg", [P, NT, NE])
        sc = sb("sc", [P, NT, NE])
        bi = xn[:, 0, :].rearrange("p (t n) -> p t n", t=NT)
        eq = xn[:, 1, :].rearrange("p (t n) -> p t n", t=NT)
        oh = [hf[:, n * NT * NE:(n + 1) * NT * NE].rearrange("p (t n) -> p t n", t=NT) for n in range(2)]
        cw = sb("cw", [P, NT, NE])
        r1 = [sb(f"r1_{n}", [P, NT]) for n in range(7)]

        bank = [ctx.enter_context(nc.psum_tensor(f"bank{n}", [P, 512], fp32)) for n in range(8)]
        S_BANK, ST_BANK, PV_BANK, A_BANK, O_BANK, T_BANK = 0, 2, 4, 5, 6, 7
        Y_BANK, Z_BANK = 6, 7
        GATE_BANK = (A_BANK, T_BANK)
        half_bank = bank[O_BANK][:, 0:S]

        x_in = [sem(f"x_in{n}") for n in range(4)]
        c_in = sem("c_in")
        w4_in = sem("w4_in")
        cst_in = sem("cst_in")
        w13_in = sem("w13_in")
        small_in = sem("small_in")
        w2_in = sem("w2_in")
        dram_out = sem("dram_out")
        cw_late_out = sem("cw_late_out")
        idle_zero = sem("idle_zero")
        b2_zero = sem("b2_zero")
        wsplit = sem("wsplit")
        wrep_done = sem("wrep_done")
        silu_sig = sem("silu_sig")
        silu_done = sem("silu_done")
        mod_mm = sem("mod_mm")
        mod_done = sem("mod_done")
        ga_mm = sem("ga_mm")
        g_chain = sem("g_chain")
        gaB_ready = sem("gaB_ready")
        ga_ready = sem("ga_ready")
        gb_ready = sem("gb_ready")
        gwsplit = sem("gwsplit")
        w13hi = sem("w13hi")
        w13lo = sem("w13lo")
        st1_done = sem("st1_done")
        mv1_done = sem("mv1_done")
        std_in = sem("std_in")
        std_done = sem("std_done")
        rstd_done = sem("rstd_done")
        xn_ready = sem("xn_ready")
        xnT_done = sem("xnT_done")
        h_ready = sem("h_ready")
        hl_ready = sem("hl_ready")
        qk_mm = sem("qk_mm")
        hi_ready = sem("hi_ready")
        stage_ready = sem("stage_ready")
        copied = sem("copied")
        s_mm = sem("s_mm")
        max_done = sem("max_done")
        mT_done = sem("mT_done")
        m_split = sem("m_split")
        mrow = [sem(f"mrow{n}") for n in range(2)]
        st_mm = sem("st_mm")
        exp_done = sem("exp_done")
        v_mm = sem("v_mm")
        v_ready = sem("v_ready")
        pv_mm = sem("pv_mm")
        ot_ready = sem("ot_ready")
        otr_mm = sem("otr_mm")
        rd_ready = sem("rd_ready")
        cc_ready = sem("cc_ready")
        cT_mm = sem("cT_mm")
        cch_ready = sem("cch_ready")
        ccl_ready = sem("ccl_ready")
        o_mm = sem("o_mm")
        rt_ready = sem("rt_ready")
        x2_ready = sem("x2_ready")
        st2_done = sem("st2_done")
        mv2_done = sem("mv2_done")
        std2_in = sem("std2_in")
        std2_done = sem("std2_done")
        rstd2_done = sem("rstd2_done")
        xn2_ready = sem("xn2_ready")
        x2T_done = sem("x2T_done")
        h2_ready = sem("h2_ready")
        h2l_ready = sem("h2l_ready")
        gate_mm = sem("gate_mm")
        lg_ready = sem("lg_ready")
        route = sem("route")
        exp_gate = sem("exp_gate")
        cw_done = sem("cw_done")
        cwT_zero = sem("cwT_zero")
        cwT_mm = sem("cwT_mm")
        cwT_done = sem("cwT_done")
        cwB_in = [sem(f"cwB_in{n}") for n in range(R)]
        g_mm = sem("g_mm")
        l_mm = sem("l_mm")
        t1g_ready = sem("t1g_ready")
        t1l_ready = sem("t1l_ready")
        pg_ready = sem("pg_ready")
        gm_ready = sem("gm_ready")
        pl_ready = sem("pl_ready")
        lc_ready = sem("lc_ready")
        sg_ready = sem("sg_ready")
        x_ready = sem("x_ready")
        yx_ready = sem("yx_ready")
        a_ready = sem("a_ready")
        last_a_ready = sem("last_a_ready")
        w2_mm = sem("w2_mm")
        z_ready = sem("z_ready")
        zT_done = sem("zT_done")
        yo_ready = sem("yo_ready")

        def x2_bank(c):
            return S_BANK + c % 2 if c < EARLY else T_BANK

        def later(value):
            return not isinstance(value, int) or value > 0

        block = ctx.enter_context(nc.Block())

        def x_before(c, n):
            return NE * c + (n - R if n >= R else n - R + 1)

        def bodies(e, body):
            for b in range(-2, 2):
                body(b, b % 2)
            with e.Fori(0, (NB - 4) // 2) as i:
                body(2 * i + 2, 0)
                body(2 * i + 3, 1)
            for b in range(NB - 2, NB):
                body(b, b % 2)

        def has(b, stage_of):
            return not isinstance(b, int) or 0 <= b + stage_of < NB

        def early(b):
            return isinstance(b, int) and b == -1

        def a_bank(b, n):
            if isinstance(b, int) and b < 2:
                return bank[((A_BANK, PV_BANK, O_BANK, T_BANK), (A_BANK, PV_BANK, ST_BANK, ST_BANK + 1))[b][n]]
            return bank[A_BANK]

        def o_bank(b, qt):
            return T_BANK if isinstance(b, int) and b == NB - 1 and qt == 1 else O_BANK

        def out_psum(b):
            if isinstance(b, int) and b == NB - 1:
                return bank[T_BANK][:, TB * P:TB * P + TB * D]
            return bank[O_BANK][:, 0:TB * D]

        FIRST = 4
        EARLY = NC - 1
        part_tiles = [slice(0, EARLY * CT), slice(EARLY * CT, NT)]
        CWT_BANK = (A_BANK, O_BANK, T_BANK, T_BANK)

        @block.sync
        def _(sp):
            sp.dma_start(cT[:], cT_d).then_inc(c_in, DMA)
            q = NT // 4
            for n in range(4):
                sp.dma_start(xs[:, n * q:(n + 1) * q, :], x_d[:, n * q:(n + 1) * q, :]).then_inc(x_in[n], DMA)
                if n == 0:
                    sp.dma_start(wmod, wmod_d).then_inc(c_in, DMA)
                    sp.dma_start(w4[:], w4_d).then_inc(w4_in, DMA)
                    for dst, src in ((ident, ident_d), (cols, cols_d), (rev, rev_d)):
                        sp.dma_start(dst[:], src).then_inc(cst_in, DMA)
            sp.wait_ge(b2_zero, 1)
            sp.dma_start(b2[0:NE, :], b2_d).then_inc(small_in, DMA)
            sp.dma_start(sb2[:], sb2_d).then_inc(small_in, DMA)
            sp.dma_start(gwT[:], gw_d).then_inc(small_in, DMA)
            sp.dma_start(gbb[:], gb_d.partition_broadcast(P)).then_inc(small_in, DMA)
            sp.dma_start(b13[:], b13_d).then_inc(small_in, DMA)
            sp.dma_start(w13, w13_d).then_inc(w13_in, DMA)
            sp.dma_start(w2[:], w2_d).then_inc(w2_in, DMA)

            def maxima_rows(b, par, half):
                sp.wait_ge(m_split, 4 * b + 2 * half + 2)
                for part in range(2):
                    for g2 in range(2):
                        sp.dma_start(Qst[par][24 + part:P:32, 2 * half + g2, :].bitcast(fp32),
                                    mhl[J * g2:J * g2 + J, half, part, :].bitcast(fp32)).then_inc(mrow[half], DMA)

            def body(b, par):
                if has(b, 0):
                    maxima_rows(b, par, 1)
                if has(b, 1):
                    maxima_rows(b + 1, 1 - par, 0)

            bodies(sp, body)

            sp.wait_ge(cwT_done, EARLY)
            sp.dma_start(cwd[:, 0:EARLY * CW], cwT[0:NE, 0:EARLY * CW]).then_inc(dram_out, DMA)
            sp.wait_ge(dram_out, DMA)

            def chunk(c):
                for n in range(1, NX):
                    r = n % R
                    if later(x_before(c, n)):
                        sp.wait_ge(x_ready, x_before(c, n))
                    sp.dma_start(cwB[:, r, :], cwd[n - 1, bass.ds(c * CW, CW)].partition_broadcast(P))\
                     .then_inc(cwB_in[r], DMA)

            def store(c):
                sp.wait_ge(yo_ready, c + 1)
                sp.dma_start(y_d[:, bass.ds(c * CT, CT), :], yo).then_inc(dram_out, DMA)

            chunk(0)
            with sp.Fori(1, NC) as c:
                chunk(c)
                sp.wait_ge(cw_late_out, DMA)
                store(c - 1)
            store(NC - 1)
            sp.wait_ge(dram_out, (NC + 1) * DMA)

        @block.gpsimd
        def _(pool):
            pool.memset(zcol[:], 0.0)
            for n in range(2):
                pool.memset(V[n], 0.0).then_inc(idle_zero, 1)
            pool.wait_ge(idle_zero, 2)
            for n in range(2):
                pool.memset(V[n][:, :, :, HD:HD + 1], 1.0).then_inc(idle_zero, 1)
            pool.memset(b2[:], 0.0).then_inc(b2_zero, 1)

            def split_w13(n):
                pool.wait_ge(w13_in, DMA)
                pool.tensor_scalar(w13h[:, n, :], w13[:, n, :], 1.0, 0.0, ALU.mult, ALU.add).then_inc(w13hi, 1)
                pool.wait_ge(w13hi, n + 1)
                pool.tensor_tensor(w13l[:, n, :], w13[:, n, :], w13h[:, n, :].bitcast(fp32), ALU.subtract)\
                 .then_inc(w13lo, 1)

            def copy_group(b, par, g, reuse):
                pool.wait_ge(stage_ready, 4 * b + (2 if g < 2 else 4))
                if reuse:
                    pool.wait_ge(st_mm, SLOTS * (b - 2) + J * g + J)
                pool.tensor_tensor(Qst[par][:, g, :], stage[:, 0, g, :].bitcast(fp32), zcol[:].to_broadcast([P, S]),
                                ALU.add)
                for j in range(J):
                    last = pool.tensor_scalar(Kx[:, par, J * g + j, :], stage[:, 1, g, :].bitcast(fp32),
                                           cols[:, 3 + j:4 + j], 0.0, ALU.mult, ALU.add)
                last.then_inc(copied, 1)

            pool.wait_ge(cst_in, 3 * DMA)

            def body(b, par):
                if has(b, 2):
                    for g in range(G):
                        copy_group(b + 2, par, g, has(b, 0))
                if isinstance(b, int) and b == NB - 2:
                    pool.wait_ge(copied, G * NB)
                    pool.memset(cwT, 0.0).then_inc(cwT_zero, 1)
                if isinstance(b, int):
                    for n in {-2: (0, 1), -1: (2,), 0: (3,), 1: (4,), NB - 2: (5, 6), NB - 1: (7, 8)}[b]:
                        split_w13(n)

            bodies(pool, body)
            pool.wait_ge(pv_mm, G * NB)

            def expert(c, n):
                r = n % R
                k = NX * c + n
                if n > 0:
                    pool.wait_ge(gm_ready, k + 1)
                    pool.wait_ge(cwB_in[r], DMA * (len(range(r or R, NX, R)) * c + len(range(r or R, n + 1, R))))
                    if later(k - R + 1):
                        pool.wait_ge(a_ready, k - R + 1)
                    pool.tensor_tensor(X[r], pg[r], cwB[:, r, :], ALU.mult).then_inc(x_ready, 1)

            def gate(c, n):
                r = n % R
                k = NX * c + n
                pool.wait_ge(yx_ready, k + 1)
                pool.wait_ge(sg_ready, k + 1)
                if later(k - R + 1):
                    pool.wait_ge(w2_mm, k - R + 1)
                pool.tensor_tensor(av[r], X[r], sg[r], ALU.mult).then_inc(a_ready, 1)

            def chunk(c):
                for n in range(NX):
                    if n > 0 or not (isinstance(c, int) and c == 0):
                        gate(c, n - 1) if n > 0 else gate(c - 1, NX - 1)
                    expert(c, n)

            chunk(0)
            with pool.Fori(1, NC) as c:
                chunk(c)

        @block.scalar
        def _(act):
            act.wait_ge(c_in, 2 * DMA)
            act.activation(sigc[:], cT[:], ACT.Sigmoid).then_inc(silu_sig, 1)
            act.wait_ge(mod_mm, 1)
            act.activation(mod[:], bank[0][:, 0:6 * NB].rearrange("p (a b) -> p a b", a=6), ACT.Identity)\
             .then_inc(mod_done, 1)
            act.wait_ge(std_in, 1)
            act.activation(std1[:, 0:FIRST], std1[:, 0:FIRST], ACT.Sqrt).then_inc(std_done, 1)

            def normalise(b):
                if isinstance(b, int) and b == 0:
                    act.wait_ge(rstd_done, 2)
                elif isinstance(b, int) and b == FIRST // TB:
                    act.wait_ge(rstd_done, 4)
                if later(b):
                    act.wait_ge(xnT_done, b)
                for k in range(TB):
                    t = TB * b + k
                    last = act.activation(xn[:, k, :], xs[:, bass.ds(t, 1), :].rearrange("p a d -> p (a d)"), ACT.Identity,
                                          bias=shift1[:, bass.ds(t, 1)], scale=rstd1[:, bass.ds(t, 1)])
                last.then_inc(xn_ready, 1)

            def maxima_hi(b, half):
                act.wait_ge(mT_done, 2 * b + half + 1)
                if later(4 * DMA * b):
                    act.wait_ge(mrow[half], 4 * DMA * b)
                act.activation(mhl[:, half, 0, :], bank[T_BANK][0:8, 0:S], ACT.Identity).then_inc(m_split, 1)

            def normed(b, par):
                act.wait_ge(xnT_done, b + 1)
                if later(b):
                    act.wait_ge(hl_ready, b)
                src = half_bank
                act.activation(hf[:], src, ACT.Identity, bias=mod[:, 0, bass.ds(b, 1)],
                             scale=mod1[:, 1, bass.ds(b, 1)]).then_inc(h_ready, 1)
                act.activation(hh[par][:], src, ACT.Identity, bias=mod[:, 0, bass.ds(b, 1)],
                             scale=mod1[:, 1, bass.ds(b, 1)]).then_inc(h_ready, 1)

            def hi_part(b, n):
                act.wait_ge(qk_mm, 4 * b + n + 1)
                if later(4 * b + n - 1):
                    act.wait_ge(stage_ready, 4 * b + n - 1)
                act.activation(hiS[n % 2][:], a_bank(b, n)[:].rearrange("p (a b) -> p a b", a=2), ACT.Identity,
                             bias=cols[:, 2:3] if n % 2 == 1 else 0.0, scale=cols[:, n % 2:n % 2 + 1])\
                 .then_inc(hi_ready, 1)

            def values(b, par):
                act.wait_ge(v_mm, b + 1)
                if later(G * (b - 1)):
                    act.wait_ge(pv_mm, G * (b - 1))
                act.activation(V[par][:, :, :, 0:HD],
                             half_bank.rearrange("p (t h d) -> p t h d", t=TB, h=H), ACT.Identity)\
                 .then_inc(v_ready, 1)

            def exps(b, i):
                u = SLOTS * b + i
                act.wait_ge(st_mm, u + 1)
                if later(G * b + i // J - 1):
                    act.wait_ge(pv_mm, G * b + i // J - 1)
                act.activation(pt[i % PE_RING], bank[ST_BANK + i % 2][:], ACT.Exp, scale=SCALE)\
                 .then_inc(exp_done, 1)

            def attended(b, par, g):
                act.wait_ge(pv_mm, G * b + g + 1)
                if g == 0 and later(TB * (b - 1)):
                    act.wait_ge(otr_mm, TB * (b - 1))
                act.activation(OT[:, par, g, :], bank[PV_BANK][:, (g % 2) * S:(g % 2 + 1) * S], ACT.Identity)\
                 .then_inc(ot_ready, 1)

            def concat_hi(b):
                act.wait_ge(cT_mm, b + 1)
                if later(b):
                    act.wait_ge(o_mm, b)
                act.activation(cch[:], bank[T_BANK][:, 0:S], ACT.Identity).then_inc(cch_ready, 1)

            def root2(part):
                act.wait_ge(std2_in, part + 1)
                act.activation(std2[:, part_tiles[part]], std2[:, part_tiles[part]], ACT.Sqrt).then_inc(std2_done, 1)

            def h2_parts(c):
                act.wait_ge(x2T_done, c + 1)
                if c >= 2:
                    act.wait_ge(h2l_ready, c - 1)
                for k in range(CW // S):
                    b = c * (CW // S) + k
                    src = bank[x2_bank(c)][:, k * S:(k + 1) * S]
                    act.activation(hf2[c % 2][:, k * S:(k + 1) * S], src, ACT.Identity, bias=mod[:, 3, b:b + 1],
                                 scale=mod1[:, 4, b:b + 1])
                    act.activation(H2h[:, c * CW + k * S:c * CW + (k + 1) * S], src, ACT.Identity,
                                 bias=mod[:, 3, b:b + 1], scale=mod1[:, 4, b:b + 1]).then_inc(h2_ready, 1)

            def gate_exp(part):
                act.wait_ge(lg_ready, part + 1)
                act.activation(sc[:, part_tiles[part]], lg[:, part_tiles[part]], ACT.Exp).then_inc(exp_gate, 1)

            def cwT_out(c):
                act.wait_ge(cwT_zero, 1)
                act.wait_ge(cwT_mm, c + 1)
                act.activation(cwT[0:NE, c * CW:(c + 1) * CW], bank[CWT_BANK[c]][0:NE, :], ACT.Identity)\
                 .then_inc(cwT_done, 1)

            act.wait_ge(cst_in, 3 * DMA)
            act.wait_ge(mod_done, 2)

            def body(b, par):
                last = isinstance(b, int) and b == NB - 1
                for i in range(SLOTS):
                    if last and i == ROOT_AT:
                        root2(0)
                    if i == 0 and has(b, 2) and not early(b):
                        normalise(b + 2)
                    if i == 11 and isinstance(b, int) and b == -2:
                        normalise(1)
                    if has(b, 0):
                        exps(b, i)
                    if i == MHI1_AT and has(b, 0):
                        maxima_hi(b, 1)
                    if i == MHI0_AT and has(b, 1):
                        maxima_hi(b + 1, 0)
                    if last and i in H2_AT:
                        h2_parts(H2_AT.index(i))
                    if last and i == GEXP_AT:
                        gate_exp(0)
                    if i == FOURTH_OUT_AT and has(b, -1):
                        attended(b - 1, 1 - par, G - 1)
                    if i == (H1_AT if early(b) else H_AT) and has(b, 2):
                        normed(b + 2, par)
                    if i in (QK1_AT if early(b) else HI_AT) and has(b, 2):
                        hi_part(b + 2, (QK1_AT if early(b) else HI_AT).index(i))
                    if i == CHI_AT and has(b, -1):
                        concat_hi(b - 1)
                    if i in ATTEND_OUT_AT and has(b, 0):
                        attended(b, par, ATTEND_OUT_AT.index(i))
                    if i == V_OUT_AT and has(b, 1):
                        if isinstance(b, int) and b == -1:
                            act.wait_ge(idle_zero, 4)
                        values(b + 1, 1 - par)
                    if i == STD_AT and early(b):
                        act.wait_ge(std_in, 2)
                        act.activation(std1[:, FIRST:NT], std1[:, FIRST:NT], ACT.Sqrt).then_inc(std_done, 1)
                    if i == GAB_AT and early(b):
                        act.wait_ge(g_chain, 5)
                        act.activation(gaB[:], gt[:, 0, :].unsqueeze(2).to_broadcast([P, NB, P]), ACT.Identity)\
                           .then_inc(gaB_ready, 1)
                    if i == GA_OUT_AT and early(b):
                        act.wait_ge(ga_mm, 1)
                        for k in range(2):
                            act.activation(ga_b[:, 4 * k:4 * k + 4, :].rearrange("p a b -> p (a b)"),
                                           bank[ST_BANK + k][:], ACT.Identity).then_inc(ga_ready, 1)

            bodies(act, body)
            attended(NB - 1, (NB - 1) % 2, G - 1)
            act.wait_ge(w13lo, NX)
            act.wait_ge(small_in, 5 * DMA)
            act.wait_ge(gb_ready, 1)

            def chunk(c):
                for n in range(NX):
                    r = n % R
                    k = NX * c + n
                    if n == 2 and not isinstance(c, int):
                        scaled(c - 1)
                    act.wait_ge(g_mm, k + 1)
                    if later(k - R + 1):
                        act.wait_ge(pg_ready, k - R + 1)
                    act.activation(t1g[r], bank[2 * ((2 * n) % R)][:], ACT.Identity, bias=b13[:, n, 0:1])\
                     .then_inc(t1g_ready, 1)
                    if n > 0 or not isinstance(c, int):
                        sigmoid(c, n - 1) if n > 0 else sigmoid(c - 1, NX - 1)
                    if isinstance(c, int):
                        beside_first_chunk(2 * n)
                    act.wait_ge(l_mm, k + 1)
                    if later(k - R + 1):
                        act.wait_ge(pl_ready, k - R + 1)
                    act.activation(t1l[r], bank[2 * ((2 * n + 1) % R)][:], ACT.Identity, bias=b13[:, n, 1:2])\
                     .then_inc(t1l_ready, 1)
                    if isinstance(c, int):
                        beside_first_chunk(2 * n + 1)

            def beside_first_chunk(half_step):
                if half_step == EARLY_CWT_OUT_BY:
                    for c in range(EARLY):
                        cwT_out(c)
                if half_step == CHI_BY:
                    concat_hi(NB - 1)
                if half_step == ROOT_BY:
                    root2(1)
                if half_step == H2_BY:
                    h2_parts(NC - 1)
                if half_step == GEXP_BY:
                    gate_exp(1)
                if half_step == CWT_OUT_BY:
                    cwT_out(NC - 1)
                    act.wait_ge(cwT_done, NC)
                    act.dma_start(cwd[:, EARLY * CW:NC * CW], cwT[0:NE, EARLY * CW:NC * CW]).then_inc(cw_late_out, DMA)

            def sigmoid(c, n):
                k = NX * c + n
                act.wait_ge(gm_ready, k + 1)
                if later(k - R + 1):
                    act.wait_ge(a_ready, k - R + 1)
                act.activation(sg[n % R], pg[n % R], ACT.Sigmoid, scale=ALPHA).then_inc(sg_ready, 1)

            def scaled(c):
                act.wait_ge(w2_mm, NX * c + NX)
                for k in range(CW // S):
                    b = c * (CW // S) + k
                    last = act.activation(zb[:, k * S:(k + 1) * S], bank[Y_BANK][:, k * S:(k + 1) * S], ACT.Identity,
                                        bias=gbias[:, bass.ds(b, 1)], scale=gb_t[:, bass.ds(b, 1)])
                last.then_inc(z_ready, 1)

            chunk(0)
            with act.Fori(1, NC) as c:
                chunk(c)
            sigmoid(NC - 1, NX - 1)
            scaled(NC - 1)

        @block.vector
        def _(dve):
            dve.wait_ge(silu_sig, 1)
            dve.tensor_tensor(siluT[:], cT[:], sigc[:], ALU.mult).then_inc(silu_done, 1)
            def stats1(tiles):
                for n in tiles:
                    if n % 4 == 0:
                        dve.wait_ge(x_in[n // 4], DMA)
                    last = dve.bn_stats(st1[:, n, :], xs[:, n, :])
                last.then_inc(st1_done, 1)

            def variances(group, tiles):
                for n in tiles:
                    last = dve.bn_aggr(mv1[:, n, :], st1[:, n, :])
                last.then_inc(mv1_done, 1)
                dve.wait_ge(mv1_done, group + 1)
                dve.tensor_scalar(std1[:, tiles[0]:NT if group else FIRST], mv1[:, tiles[0]:NT if group else FIRST, 1],
                                  EPS, None, ALU.add).then_inc(std_in, 1)

            stats1(range(FIRST))
            dve.wait_ge(st1_done, 1)
            variances(0, range(FIRST))
            dve.wait_ge(w4_in, DMA)
            dve.tensor_copy(w4h[:], w4[:]).then_inc(wsplit, 1)
            dve.memset(wrep[0][:].bitcast(fp32), 0.0)
            dve.memset(wrep[1][:].bitcast(fp32), 0.0).then_inc(wsplit, 1)
            dve.wait_ge(std_done, 1)
            dve.reciprocal(rstd1[:, 0:FIRST], std1[:, 0:FIRST]).then_inc(rstd_done, 1)
            dve.wait_ge(rstd_done, 1)

            def shift(tiles):
                dve.scalar_tensor_tensor(out=shift1[:, tiles], in0=mv1[:, tiles, 0], scalar=-1.0, in1=rstd1[:, tiles],
                                         op0=ALU.mult, op1=ALU.mult).then_inc(rstd_done, 1)

            shift(slice(0, FIRST))
            dve.wait_ge(wsplit, 2)
            dve.tensor_tensor(w4l[:], w4[:], w4h[:].bitcast(fp32), ALU.subtract).then_inc(wsplit, 1)
            dve.wait_ge(mod_done, 1)
            dve.tensor_scalar(mod1[:], mod[:], 1.0, None, ALU.add).then_inc(mod_done, 1)

            def h_lo(b, par):
                dve.wait_ge(h_ready, 2 * b + 2)
                dve.tensor_tensor(hl[par][:], hf[:], hh[par][:].bitcast(fp32), ALU.subtract).then_inc(hl_ready, 1)

            def stacked(b, n):
                dve.wait_ge(hi_ready, 4 * b + n + 1)
                if later(G * b):
                    dve.wait_ge(copied, G * b - (2 if n < 2 else 0))
                qk, half = n % 2, n // 2
                dve.tensor_tensor(stage[:, qk, 2 * half:2 * half + 2, :].rearrange("p a b -> p (a b)"), a_bank(b, n)[:],
                                  hiS[n % 2][:].bitcast(fp32).rearrange("p a b -> p (a b)"), ALU.subtract)\
                 .then_inc(stage_ready, 1)

            def maximum(b, par, i):
                u = SLOTS * b + i
                dve.wait_ge(s_mm, u + 1)
                if i == 0:
                    if later(2 * (b - 1)):
                        dve.wait_ge(mT_done, 2 * (b - 1))
                dve.tensor_reduce(out=M[:, par, i % 2, 2 * (i // 2):2 * (i // 2) + 2],
                                in_=bank[S_BANK + i % 2][:].rearrange("p (a k) -> p a k", a=2),
                                axis=AX.X, op=ALU.max, negate=True).then_inc(max_done, 1)

            def maxima_lo(b, half):
                dve.wait_ge(m_split, 4 * b + 2 * half + 1)
                dve.tensor_tensor(mhl[:, half, 1, :], bank[T_BANK][0:8, 0:S], mhl[:, half, 0, :].bitcast(fp32),
                                ALU.subtract).then_inc(m_split, 1)

            def divided(b, qt):
                dve.wait_ge(otr_mm, TB * b + qt + 1)
                if later(b):
                    dve.wait_ge(cT_mm, b)
                o = bank[o_bank(b, qt)][:].rearrange("p (h r) -> p h r", h=H)
                dve.reciprocal(rd[:, qt, :], o[:, :, HD]).then_inc(rd_ready, 1)
                dve.wait_ge(rd_ready, TB * b + qt + 1)
                dve.tensor_tensor(cc[:, qt, :].rearrange("p (h d) -> p h d", h=H), o[:, :, 0:HD],
                                rd[:, qt, :].unsqueeze(2).to_broadcast([P, H, HD]), ALU.mult).then_inc(cc_ready, 1)

            def concat_lo(b):
                dve.wait_ge(cch_ready, b + 1)
                dve.tensor_tensor(ccl[:], bank[T_BANK][:, 0:S], cch[:].bitcast(fp32), ALU.subtract)\
                 .then_inc(ccl_ready, 1)

            def residual(b):
                dve.wait_ge(o_mm, b + 1)
                dve.tensor_tensor(rt[:], out_psum(b).rearrange("p (t d) -> p t d", t=TB),
                                ga_b[:, bass.ds(b, 1), :].to_broadcast([P, TB, D]), ALU.mult)\
                 .then_inc(rt_ready, 1)
                dve.wait_ge(rt_ready, b + 1)
                xt = xs[:, bass.ds(TB * b, TB), :]
                dve.tensor_tensor(xt, rt[:], xt, ALU.add).then_inc(x2_ready, 1)

            def stats2(b):
                dve.wait_ge(x2_ready, b + 1)
                for k in range(TB):
                    t = TB * b + k
                    last = dve.bn_stats(st2[:, bass.ds(t, 1), :].rearrange("p a k -> p (a k)"),
                                      xs[:, bass.ds(t, 1), :].rearrange("p a d -> p (a d)"))
                last.then_inc(st2_done, 1)

            def guards(step):
                g = mod[:, 2:6:3, :]
                if step == 0:
                    dve.tensor_scalar(gneg[:], g, -1.0, None, ALU.mult).then_inc(g_chain, 1)
                    dve.tensor_scalar(gsgn[:], g, 0.0, 2.0, ALU.is_ge, ALU.mult).then_inc(g_chain, 1)
                if step == 1:
                    dve.wait_ge(g_chain, 2)
                    dve.tensor_tensor(gabs[:], gneg[:], g, ALU.max).then_inc(g_chain, 1)
                if step == 2:
                    dve.wait_ge(g_chain, 3)
                    dve.tensor_scalar(gneg[:], gabs[:], 0.25, None, ALU.max).then_inc(g_chain, 1)
                if step == 3:
                    dve.wait_ge(g_chain, 4)
                    dve.scalar_tensor_tensor(out=gt[:], in0=gsgn[:], scalar=-1.0, in1=gneg[:], op0=ALU.add,
                                             op1=ALU.mult).then_inc(g_chain, 1)
                if step == 4:
                    dve.wait_ge(g_chain, 5)
                    dve.wait_ge(small_in, 5 * DMA)
                    dve.tensor_scalar(gbias[:], gb_t, sb2[:, 0:1], None, ALU.mult).then_inc(gb_ready, 1)
                    dve.tensor_copy(gwh[:], gwT[:]).then_inc(gwsplit, 1)
                if step == 5:
                    dve.wait_ge(gwsplit, 1)
                    dve.tensor_tensor(gwl[:], gwT[:], gwh[:].bitcast(fp32), ALU.subtract).then_inc(gwsplit, 1)

            def replicated():
                dve.wait_ge(wsplit, 3)
                for n, w in enumerate((w4h, w4l)):
                    for c in range(3):
                        last = dve.tensor_copy(wrep[n][:, :, :, c, :],
                                               w[:, 0:2, :].bitcast(fp32).rearrange("p a (h d) -> p a h d", h=H))
                last.then_inc(wrep_done, 1)

            def variances2(part):
                rows = (EARLY * CW, NC * CW)[part] // S
                dve.wait_ge(st2_done, rows)
                for t in range(NT)[part_tiles[part]]:
                    last = dve.bn_aggr(mv2[:, t, :], st2[:, t, :])
                last.then_inc(mv2_done, 1)
                dve.wait_ge(mv2_done, part + 1)
                dve.tensor_scalar(std2[:, part_tiles[part]], mv2[:, part_tiles[part], 1], EPS, None, ALU.add)\
                 .then_inc(std2_in, 1)

            def inverse2(part):
                dve.wait_ge(std2_done, part + 1)
                dve.reciprocal(rstd2[:, part_tiles[part]], std2[:, part_tiles[part]]).then_inc(rstd2_done, 1)
                dve.wait_ge(rstd2_done, part + 1)

            def normalise2(c):
                if c >= 2:
                    dve.wait_ge(x2T_done, c - 1)
                for k in range(CT):
                    t = c * CT + k
                    last = dve.tensor_scalar(xn2[c % 2][:, k * P:(k + 1) * P], xs[:, t, :], mv2[:, t, 0:1],
                                           rstd2[:, t:t + 1], ALU.subtract, ALU.mult)
                last.then_inc(xn2_ready, 1)

            def h2_lo(c):
                dve.wait_ge(h2_ready, 2 * c + 2)
                dve.tensor_tensor(H2l[:, c * CW:(c + 1) * CW], hf2[c % 2],
                                H2h[:, c * CW:(c + 1) * CW].bitcast(fp32), ALU.subtract).then_inc(h2l_ready, 1)

            step = [0]

            def link(ins):
                step[0] += 1
                ins.then_inc(route, 1)
                dve.wait_ge(route, step[0])

            def per_token(v, T):
                return v[:, T].unsqueeze(2).to_broadcast([P, T.stop - T.start, NE])

            def per_expert(v, T):
                return v[:].unsqueeze(1).to_broadcast([P, T.stop - T.start, NE])

            def logits_less_max(part):
                T = part_tiles[part]
                dve.wait_ge(gate_mm, part + 1)
                logits = bank[GATE_BANK[part]][:, T.start * NE:T.stop * NE].rearrange("p (t n) -> p t n", n=NE)
                link(dve.tensor_reduce(out=r1[0][:, T], in_=logits, axis=AX.X, op=ALU.max))
                dve.tensor_tensor(lg[:, T], logits, per_token(r1[0], T), ALU.subtract).then_inc(lg_ready, 1)

            def expert_scores(part):
                T = part_tiles[part]
                dve.wait_ge(exp_gate, part + 1)
                link(dve.tensor_reduce(out=r1[1][:, T], in_=sc[:, T], axis=AX.X, op=ALU.add))
                link(dve.reciprocal(r1[2][:, T], r1[1][:, T]))
                link(dve.tensor_tensor(lg[:, T], sc[:, T], per_token(r1[2], T), ALU.mult))
                link(dve.tensor_tensor(bi[:, T], lg[:, T], per_expert(gbb, T), ALU.add))

            def top(part, n):
                T = part_tiles[part]
                value, index = r1[3 + 2 * n], r1[4 + 2 * n]
                if n == 1:
                    link(dve.scalar_tensor_tensor(out=bi[:, T], in0=oh[0][:, T], scalar=-3.0e38, in1=bi[:, T],
                                                op0=ALU.mult, op1=ALU.add))
                link(dve.tensor_reduce(out=value[:, T], in_=bi[:, T], axis=AX.X, op=ALU.max))
                link(dve.tensor_tensor(eq[:, T], bi[:, T], per_token(value, T), ALU.is_ge))
                link(dve.tensor_tensor(cw[:, T], eq[:, T], per_expert(rev, T), ALU.mult))
                link(dve.tensor_reduce(out=index[:, T], in_=cw[:, T], axis=AX.X, op=ALU.max))
                link(dve.tensor_tensor(oh[n][:, T], cw[:, T], per_token(index, T), ALU.is_equal))

            def expert_weights(part):
                T = part_tiles[part]
                link(dve.tensor_tensor(eq[:, T], oh[0][:, T], oh[1][:, T], ALU.add))
                dve.tensor_tensor(cw[:, T], eq[:, T], lg[:, T], ALU.mult).then_inc(cw_done, 1)

            dve.wait_ge(cst_in, 3 * DMA)

            def body(b, par):
                last = isinstance(b, int) and b == NB - 1
                for i in range(SLOTS):
                    if has(b, 1):
                        maximum(b + 1, 1 - par, i)
                    if isinstance(b, int) and b == -2:
                        if i == 0:
                            replicated()
                    if isinstance(b, int) and b == -1:
                        if i == RSTD_AT:
                            dve.wait_ge(std_done, 2)
                            dve.reciprocal(rstd1[:, FIRST:NT], std1[:, FIRST:NT]).then_inc(rstd_done, 1)
                            dve.wait_ge(rstd_done, 3)
                            shift(slice(FIRST, NT))
                        guards(i - GUARD_AT)
                    if i == PARTS1_AT and has(b, 0):
                        maxima_lo(b, 1)
                    if i == (HL1_AT if early(b) else HL_AT) and has(b, 2):
                        h_lo(b + 2, par)
                    if i in DIV_AT and has(b, -1):
                        divided(b - 1, DIV_AT.index(i))
                    if i in (STACK1_AT if early(b) else STACK_AT) and has(b, 2):
                        stacked(b + 2, (STACK1_AT if early(b) else STACK_AT).index(i))
                    if isinstance(b, int) and b == -2 and i == 4:
                        stats1(range(FIRST, NT))
                    if isinstance(b, int) and b == -2 and i == SLOTS - 1:
                        dve.wait_ge(st1_done, 2)
                        variances(1, range(FIRST, NT))
                    if i == CLO_AT and has(b, -1):
                        concat_lo(b - 1)
                    if i == PARTS0_AT and has(b, 1):
                        maxima_lo(b + 1, 0)
                    if i == RES_AT and has(b, -1):
                        residual(b - 1)
                    if i == ST2_AT and has(b, -2):
                        stats2(b - 2)
                    if last and i == VAR_AT:
                        variances2(0)
                    if last and i == XN2_AT[0]:
                        inverse2(0)
                    if last and i in XN2_AT:
                        normalise2(XN2_AT.index(i))
                    if last and i in H2L_AT:
                        h2_lo(H2L_AT.index(i))
                    if last and i == LOG_AT:
                        logits_less_max(0)
                    if last and i == TOP_AT:
                        expert_scores(0)
                        top(0, 0)
                        top(0, 1)
                        expert_weights(0)

            bodies(dve, body)

            def chunk(c):
                for n in range(NX):
                    r = n % R
                    k = NX * c + n
                    dve.wait_ge(t1g_ready, k + 1)
                    if later(k - R + 1):
                        dve.wait_ge(sg_ready, k - R + 1)
                    if later(x_before(c, n)):
                        dve.wait_ge(x_ready, x_before(c, n))
                    dve.scalar_tensor_tensor(out=pg[r], in0=bank[2 * ((2 * n) % R) + 1][:], scalar=b13[:, n, 2:3],
                                           in1=t1g[r], op0=ALU.add, op1=ALU.mult).then_inc(pg_ready, 1)
                    dve.wait_ge(pg_ready, k + 1)
                    dve.tensor_scalar(pg[r], pg[r], LIMIT, None, ALU.min).then_inc(gm_ready, 1)
                    if n > 0 or not isinstance(c, int):
                        weighted(c, n - 1) if n > 0 else weighted(c - 1, NX - 1)
                    if isinstance(c, int):
                        beside_first_chunk(2 * n)
                    dve.wait_ge(t1l_ready, k + 1)
                    dve.scalar_tensor_tensor(out=pl[r], in0=bank[2 * ((2 * n + 1) % R) + 1][:], scalar=b13[:, n, 3:4],
                                           in1=t1l[r], op0=ALU.add, op1=ALU.mult).then_inc(pl_ready, 1)
                    dve.wait_ge(pl_ready, k + 1)
                    dve.tensor_scalar(pl[r], pl[r], -LIMIT, LIMIT, ALU.max, ALU.min).then_inc(lc_ready, 1)
                    if n == 4 and not isinstance(c, int):
                        finish(c - 1)
                    if isinstance(c, int):
                        beside_first_chunk(2 * n + 1)

            def beside_first_chunk(half_step):
                if half_step == DIV_BY:
                    divided(NB - 1, 0)
                    divided(NB - 1, 1)
                if half_step == CLO_BY:
                    concat_lo(NB - 1)
                if half_step == RES_BY:
                    residual(NB - 1)
                    stats2(NB - 2)
                    stats2(NB - 1)
                if half_step == VAR_BY:
                    variances2(1)
                if half_step == XN2_BY:
                    inverse2(1)
                    normalise2(NC - 1)
                if half_step == H2L_BY:
                    h2_lo(NC - 1)
                if half_step == LOG_BY:
                    logits_less_max(1)
                if half_step == SCORE_BY:
                    expert_scores(1)
                    top(1, 0)
                if half_step == TOP_BY:
                    top(1, 1)
                    expert_weights(1)

            def weighted(c, n):
                r = n % R
                k = NX * c + n
                dve.wait_ge(lc_ready, k + 1)
                if n > 0:
                    dve.wait_ge(x_ready, NE * c + n)
                else:
                    if later(k - R + 1):
                        dve.wait_ge(a_ready, k - R + 1)
                dve.scalar_tensor_tensor(out=X[r], in0=pl[r], scalar=1.0, in1=X[r] if n > 0 else pg[r],
                                       op0=ALU.add, op1=ALU.mult).then_inc(yx_ready, 1)

            def finish(c):
                dve.wait_ge(zT_done, c + 1)
                dve.wait_ge(dram_out, DMA * (c + 1))
                dve.tensor_tensor(yo, bank[Z_BANK][:].rearrange("p (t d) -> p t d", t=CT),
                                xs[:, bass.ds(c * CT, CT), :], ALU.add).then_inc(yo_ready, 1)

            dve.wait_ge(w13lo, NX)
            dve.wait_ge(pv_mm, G * NB)
            chunk(0)
            with dve.Fori(1, NC) as c:
                chunk(c)
            weighted(NC - 1, NX - 1)
            dve.wait_ge(yx_ready, NX * NC)
            dve.wait_ge(sg_ready, NX * NC)
            dve.wait_ge(w2_mm, NX * NC - R)
            dve.tensor_tensor(av[(NX - 1) % R], X[(NX - 1) % R], sg[(NX - 1) % R], ALU.mult)\
               .then_inc(last_a_ready, 1)
            finish(NC - 1)

        @block.tensor
        def _(pe):
            def product(out, hi, lo, rhi, rlo):
                pe.matmul(out, hi, rhi, start=True, stop=False)
                pe.matmul(out, lo, rhi, start=False, stop=False)
                return pe.matmul(out, hi, rlo, start=False, stop=True)

            pe.wait_ge(silu_done, 1)
            pe.wait_ge(c_in, 2 * DMA)
            for k in range(6):
                last = pe.matmul(bank[0][:, k * NB:(k + 1) * NB], wmod[:, k, :], siluT[:], start=True, stop=True)
            last.then_inc(mod_mm, 1)

            def normedT(b):
                pe.wait_ge(xn_ready, b + 1)
                if later(b - 1):
                    pe.wait_ge(v_ready, b - 1)
                if later(b - 3):
                    pe.wait_ge(rt_ready, b - 3)
                if isinstance(b, int) and b == 1:
                    pe.wait_ge(stage_ready, 4)
                for k in range(TB):
                    last = pe.transpose(half_bank[:, k * P:(k + 1) * P], xn[:, k, :], ident[:])
                last.then_inc(xnT_done, 1)

            def qk_step(b, par, n, k):
                pe.wait_ge(hl_ready, b + 1)
                if k == 0 and not (isinstance(b, int) and b < 2):
                    pe.wait_ge(stage_ready, 4 * b + n)
                qk, half = n % 2, n // 2
                g = 2 * half + k
                wh = wrep[0][:, qk, J * g:J * g + J].rearrange("p h c d -> p (h c d)")
                wl = wrep[1][:, qk, J * g:J * g + J].rearrange("p h c d -> p (h c d)")
                last = product(a_bank(b, n)[:, k * S:(k + 1) * S], wh, wl, hh[par][:], hl[par][:])
                if k == 1:
                    last.then_inc(qk_mm, 1)

            def values(b, par):
                if later(TB * (b - 1)):
                    pe.wait_ge(cc_ready, TB * (b - 1))
                elif b + 1 < NB:
                    pe.wait_ge(h_ready, 2 * (b + 2))
                for k in range(TB):
                    tk = slice(k * P, (k + 1) * P)
                    last = product(half_bank[:, k * D:(k + 1) * D], hh[par][:, tk], hl[par][:, tk],
                                   w4h[:, 2, :], w4l[:, 2, :])
                last.then_inc(v_mm, 1)

            def scores_q(b, par, i):
                u = SLOTS * b + i
                pair, qt = i // 2, i % 2
                g = pair // 2
                if i % 4 == 0:
                    pe.wait_ge(copied, G * b + g + 1)
                if later(u - 1):
                    pe.wait_ge(max_done, u - 1)
                pe.matmul(bank[S_BANK + i % 2][:], Qst[par][:, g, qt * P:(qt + 1) * P],
                         Kx[:, par, 2 * pair:2 * pair + 2, :].rearrange("p a b -> p (a b)"),
                         start=True, stop=True).then_inc(s_mm, 1)

            def scores_k(b, par, h):
                u = SLOTS * b + h
                if h % (H // 2) == 0:
                    pe.wait_ge(mrow[h // (H // 2)], 4 * DMA * (b + 1))
                if isinstance(u, int) and u == 0:
                    pe.wait_ge(ga_ready, 2)
                if later(u - 1):
                    pe.wait_ge(exp_done, u - 1)
                for k in range(TB):
                    last = pe.matmul(bank[ST_BANK + h % 2][:, k * S:(k + 1) * S], Kx[:, par, h, k * P:(k + 1) * P],
                                    Qst[par][:, h // J, :], start=True, stop=True)
                last.then_inc(st_mm, 1)

            def attend(b, par, g, part):
                if part == 0:
                    pe.wait_ge(exp_done, SLOTS * b + J * g + J)
                    pe.wait_ge(v_ready, b + 1)
                    if later(G * b + g - 1):
                        pe.wait_ge(ot_ready, G * b + g - 1)
                for k in range(part * TB // 2, (part + 1) * TB // 2):
                    for j in range(J):
                        h = J * g + j
                        last = pe.matmul(bank[PV_BANK][32 * j:32 * j + 32, (g % 2) * S:(g % 2 + 1) * S],
                                        V[par][:, k, h, :], pt[h % PE_RING][:, k * S:(k + 1) * S],
                                        start=k == 0, stop=k == TB - 1, skip_group_check=True)
                if part == 1:
                    last.then_inc(pv_mm, 1)

            def maximaT(b, par, half):
                pe.wait_ge(max_done, SLOTS * b + 8 * half + 8)
                if half == 1:
                    pe.wait_ge(m_split, 4 * b + 2)
                    if later(b - 1):
                        pe.wait_ge(ccl_ready, b - 1)
                elif not (isinstance(b, int) and b == 0):
                    pe.wait_ge(m_split, 4 * b)
                for k in range(TB):
                    last = pe.transpose(bank[T_BANK][0:8, k * P:(k + 1) * P],
                                       M[:, par, k, 8 * half:8 * half + 8], ident[:])
                last.then_inc(mT_done, 1)

            def attendedT(b, par, qt):
                pe.wait_ge(ot_ready, G * b + G)
                if later(b):
                    pe.wait_ge(rt_ready, b)
                if not isinstance(b, int) or b + 3 < NB:
                    pe.wait_ge(h_ready, 2 * (b + 4))
                if isinstance(b, int) and b == NB - 1:
                    pe.wait_ge(cwT_done, EARLY)
                elif later(TB * b + qt):
                    pe.wait_ge(cc_ready, TB * b + qt)
                for g in range(G):
                    last = pe.transpose(bank[o_bank(b, qt)][:, g * P:(g + 1) * P], OT[:, par, g, qt * P:(qt + 1) * P], ident[:])
                last.then_inc(otr_mm, 1)

            def concatT(b):
                pe.wait_ge(cc_ready, TB * b + TB)
                if later(b):
                    pe.wait_ge(ccl_ready, b)
                if isinstance(b, int) and b == NB - 2:
                    pe.wait_ge(m_split, 4 * NB)
                elif not (isinstance(b, int) and b == NB - 1):
                    pe.wait_ge(m_split, 4 * (b + 2) + 2)
                for k in range(TB):
                    last = pe.transpose(bank[T_BANK][:, k * P:(k + 1) * P], cc[:, k, :], ident[:])
                last.then_inc(cT_mm, 1)

            def output(b):
                pe.wait_ge(ccl_ready, b + 1)
                if not isinstance(b, int) or b + 2 < NB:
                    pe.wait_ge(v_ready, b + 3)
                for k in range(TB):
                    tk = slice(k * P, (k + 1) * P)
                    last = product(out_psum(b)[:, k * D:(k + 1) * D], cch[:, tk], ccl[:, tk],
                                   w4h[:, 3, :], w4l[:, 3, :])
                last.then_inc(o_mm, 1)

            def normed2T(c):
                pe.wait_ge(xn2_ready, c + 1)
                if c == 0:
                    pe.wait_ge(max_done, SLOTS * NB)
                if c >= 2:
                    pe.wait_ge(h2_ready, 2 * (c - 1))
                for k in range(CT):
                    last = pe.transpose(bank[x2_bank(c)][:, k * P:(k + 1) * P], xn2[c % 2][:, k * P:(k + 1) * P],
                                        ident[:])
                last.then_inc(x2T_done, 1)

            def gate(c):
                if c == 0:
                    pe.wait_ge(stage_ready, 4 * NB)
                    pe.wait_ge(gwsplit, 2)
                pe.wait_ge(h2l_ready, c + 1)
                for k in range(CT):
                    t = c * CT + k
                    tk = slice(t * P, (t + 1) * P)
                    last = product(bank[GATE_BANK[c // EARLY]][:, t * NE:(t + 1) * NE], H2h[:, tk], H2l[:, tk],
                                   gwh[:], gwl[:])
                if c >= EARLY - 1:
                    last.then_inc(gate_mm, 1)

            def cwT_chunk(c):
                if c == 1:
                    pe.wait_ge(rt_ready, NB - 1)
                for k in range(CT):
                    last = pe.transpose(bank[CWT_BANK[c]][0:NE, k * P:(k + 1) * P], cw[:, c * CT + k, :], ident[:])
                last.then_inc(cwT_mm, 1)

            pe.wait_ge(cst_in, 3 * DMA)

            def body(b, par):
                last_body = isinstance(b, int) and b == NB - 1
                for i in range(SLOTS):
                    if has(b, 1):
                        scores_q(b + 1, 1 - par, i)
                    if has(b, 0):
                        scores_k(b, par, i)
                    if i == FOURTH_AT and has(b, -1):
                        attend(b - 1, 1 - par, G - 1, 0)
                    if i == FOURTHB_AT and has(b, -1):
                        attend(b - 1, 1 - par, G - 1, 1)
                    if i == MAXT1_AT and has(b, 0):
                        maximaT(b, par, 1)
                    if i == 3 and isinstance(b, int) and b == -2:
                        pe.wait_ge(wrep_done, 1)
                    if i == GA_AT and early(b):
                        pe.wait_ge(gaB_ready, 1)
                        pe.wait_ge(stage_ready, 8)
                        for k in range(NB):
                            last = pe.matmul(bank[ST_BANK + k // 4][:, (k % 4) * D:(k % 4 + 1) * D], gaB[:, k, :],
                                             ident[:], start=True, stop=True)
                        last.then_inc(ga_mm, 1)
                    if i == (XNT1_AT if early(b) else XNT_AT) and has(b, 2):
                        normedT(b + 2)
                    if i in OT_AT and has(b, -1):
                        attendedT(b - 1, 1 - par, OT_AT.index(i))
                    if i in (QK1_AT if early(b) else QK_AT) and has(b, 2):
                        qk_step(b + 2, par, (QK1_AT if early(b) else QK_AT).index(i), 0)
                    if i in (QK1_AT if early(b) else QKB_AT) and has(b, 2):
                        qk_step(b + 2, par, (QK1_AT if early(b) else QKB_AT).index(i), 1)
                    if i in ATTEND_AT and has(b, 0):
                        attend(b, par, ATTEND_AT.index(i), 0)
                    if i in ATTENDB_AT and has(b, 0):
                        attend(b, par, ATTENDB_AT.index(i), 1)
                    if i == CT_AT and has(b, -1):
                        concatT(b - 1)
                    if i == OUT_AT and has(b, -1):
                        output(b - 1)
                    if i == MAXT0_AT and has(b, 1):
                        maximaT(b + 1, 1 - par, 0)
                    if i == V_AT and has(b, 1):
                        values(b + 1, 1 - par)
                    if last_body and i in X2T_AT:
                        normed2T(X2T_AT.index(i))
                    if last_body and i in GATE_AT:
                        gate(GATE_AT.index(i))

            bodies(pe, body)
            attend(NB - 1, (NB - 1) % 2, G - 1, 0)
            attend(NB - 1, (NB - 1) % 2, G - 1, 1)

            def first_layer(c, n):
                rhi, rlo = H2h[:, bass.ds(c * CW, CW)], H2l[:, bass.ds(c * CW, CW)]
                for part, done in ((0, g_mm), (1, l_mm)):
                    u = 2 * n + part
                    prev = u - R
                    k = NX * c + prev // 2
                    if isinstance(c, int) and u == 1:
                        pe.wait_ge(exp_done, SLOTS * NB)
                    if isinstance(c, int) and u == 2:
                        pe.wait_ge(ot_ready, G * NB)
                        pe.wait_ge(cwT_done, 1)
                    if later(k + 1) and prev % 2:
                        pe.wait_ge(pl_ready, k + 1)
                    elif later(k + 1):
                        pe.wait_ge(pg_ready, k + 1)
                    for m in range(2):
                        w = slice((2 * m + part) * P, (2 * m + part + 1) * P)
                        last = product(bank[2 * (u % R) + m][:], w13h[:, n, w], w13l[:, n, w], rhi, rlo)
                    last.then_inc(done, 1)
                    if isinstance(c, int):
                        beside_first_chunk(u)

            def second_layer(c, n):
                if n == 0:
                    if later(c):
                        pe.wait_ge(z_ready, c)
                    pe.matmul(bank[Y_BANK][:], b2[:], cwT[:, bass.ds(c * CW, CW)], start=True, stop=False)
                if isinstance(c, int) and (c, n) == (NC - 1, NX - 1):
                    pe.wait_ge(last_a_ready, 1)
                else:
                    pe.wait_ge(a_ready, NX * c + n + 1)
                last = pe.matmul(bank[Y_BANK][:], w2[:, n, :], av[n % R], start=False, stop=n == NX - 1)
                last.then_inc(w2_mm, 1)

            def backT(c):
                pe.wait_ge(z_ready, c + 1)
                for k in range(CT):
                    last = pe.transpose(bank[Z_BANK][:, k * P:(k + 1) * P], zb[:, k * P:(k + 1) * P], ident[:])
                last.then_inc(zT_done, 1)

            LAG = 2

            def beside_first_chunk(half_step):
                if half_step == EARLY_CWT_BY:
                    pe.wait_ge(cw_done, 1)
                    for c in range(EARLY):
                        cwT_chunk(c)
                if half_step == OT_BY:
                    attendedT(NB - 1, (NB - 1) % 2, 0)
                    attendedT(NB - 1, (NB - 1) % 2, 1)
                if half_step == CT_BY:
                    concatT(NB - 1)
                if half_step == OUT_BY:
                    output(NB - 1)
                if half_step == X2T_BY:
                    normed2T(NC - 1)
                if half_step == GATE_BY:
                    gate(NC - 1)
                if half_step == CWT_BY:
                    pe.wait_ge(cw_done, 2)
                    cwT_chunk(NC - 1)

            def chunk(c):
                for n in range(NX):
                    first_layer(c, n)
                    if n >= LAG:
                        second_layer(c, n - LAG)
                    elif not isinstance(c, int):
                        second_layer(c - 1, NX + n - LAG)
                    if n == 3 and not isinstance(c, int):
                        backT(c - 1)

            pe.wait_ge(w13lo, NX)
            pe.wait_ge(w2_in, DMA)
            pe.wait_ge(small_in, 5 * DMA)
            chunk(0)
            with pe.Fori(1, NC) as c:
                chunk(c)
            for n in range(NX - LAG, NX):
                second_layer(NC - 1, n)
            backT(NC - 1)


def kernel(**inputs):
    import numpy as np
    import concourse.bacc as _bacc
    from concourse import mybir as _mybir
    from concourse.bass_utils import run_bass_kernel_spmd as _run

    a = {k: np.asarray(v) for k, v in inputs.items()}
    x = a["L0_attn_x"]
    B, S, D = x.shape
    P = 128
    NT = B * S // P
    x_l = x.reshape(NT, P, D).transpose(1, 0, 2)
    w4 = np.stack([a["L0_attn_w_" + n].T for n in "qkvo"], axis=1)
    E, F2, _ = a["L0_ffn_w1"].shape
    w1 = np.concatenate([a["L0_ffn_sw1"][None], a["L0_ffn_w1"]])
    w3 = np.concatenate([a["L0_ffn_sw3"][None], a["L0_ffn_w3"]])
    w13 = np.concatenate([w1[:, 0::2], w1[:, 1::2], w3[:, 0::2], w3[:, 1::2]], axis=1).transpose(2, 0, 1)
    b1 = np.concatenate([a["L0_ffn_sb1"][None], a["L0_ffn_b1"]])
    b3 = np.concatenate([a["L0_ffn_sb3"][None], a["L0_ffn_b3"]])
    b13 = np.stack([b1[:, 0::2], b1[:, 1::2], b3[:, 0::2], b3[:, 1::2]], axis=1).transpose(2, 0, 1)
    w2 = np.concatenate([a["L0_ffn_sw2"][None], a["L0_ffn_w2"]]).transpose(2, 0, 1)
    row = np.arange(P) % 32
    c = row // 8
    one = row // 2 == 12
    cols = np.stack([np.where(c == 1, 1.0, 0.0), np.where(c == 2, 1.0, 0.0), np.where(one, -1.0, 0.0)] + [np.where(np.arange(P) // 32 == j, 1.0, 0.0) for j in range(4)],
                    axis=1).astype(np.float32)
    ins = {
        "x": x_l, "w4": w4, "cT": a["L0_c"].T, "wmod": a["L0_wmod"].reshape(D, 6, D), "w13": w13, "w2": w2,
        "b13": b13, "b2": a["L0_ffn_b2"], "sb2": a["L0_ffn_sb2"].reshape(D, 1), "gw": a["L0_ffn_gate_w"].T,
        "gb": a["L0_ffn_gate_b"], "ident": np.eye(P, dtype=np.float32), "cols": cols,
        "rev": np.ascontiguousarray(np.broadcast_to(np.arange(E, 0, -1, dtype=np.float32), (P, E))),
    }
    nc = _bacc.Bacc("TRN2", target_bir_lowering=False, num_devices=1)
    arrays, args = {}, []
    for name, v in ins.items():
        v = np.ascontiguousarray(v)
        arrays[f"in_{name}"] = v
        args.append(nc.dram_tensor(f"in_{name}", v.shape, _mybir.dt.from_np(v.dtype), kind="ExternalInput").ap())
    args.append(nc.dram_tensor("out_y", (P, NT, D), _mybir.dt.float32, kind="ExternalOutput").ap())
    block_kernel(nc, *args)
    r = _run(nc, [arrays], core_ids=[0])
    y = r.results[0]["out_y"]
    return y.transpose(1, 0, 2).reshape(B, S, D)
```
